# Optimizing a Trainium2 kernel written in Bass

```python
import numpy as np
import jax
import jax.numpy as jnp

def _softmax(x, axis=-1):
    return jax.nn.softmax(x, axis=axis)

def _gelu(x):
    return jax.nn.gelu(x, approximate=True)

def _silu(x):
    return jax.nn.silu(x)

def _sigmoid(x):
    return jax.nn.sigmoid(x)

def _layernorm(x, axis=-1, eps=1e-05):
    m = jnp.mean(x, axis=axis, keepdims=True)
    v = jnp.var(x, axis=axis, keepdims=True)
    return (x - m) / jnp.sqrt(v + eps)

def _scatter_add(tgt, idx, src, axis=0):
    return tgt.at[idx].add(src)

def _segment_sum(src, seg, n):
    return jax.ops.segment_sum(src, seg, n)
kernel_name = 'mk_adaln_attn_ffn_d2_seqx_r8_f1a274'

def setup_inputs(seed: int=0):
    np.random.seed(seed)
    _w = jnp.asarray

    def _rec_inputs():
        import jax
        import jax.numpy as jnp
        _rk = jax.random.key(seed)
        x = -0.000125 + 0.9999 * jax.random.normal(jax.random.fold_in(_rk, 1), (4, 256, 256), jnp.float32)
        _lenS = 256 - jax.random.randint(jax.random.fold_in(_rk, 7), (4,), 0, max(1, 256 // 4) + 1, jnp.int32)
        _lenS2 = 256 - jax.random.randint(jax.random.fold_in(_rk, 8), (4,), 0, max(1, 256 // 4) + 1, jnp.int32)
        fside_BxSxS_0 = -1.52775e-05 + 0.999936 * jax.random.normal(jax.random.fold_in(_rk, 11), (4, 256, 256), jnp.float32)
        cond_512 = -5.03954e-05 + 1.00559 * jax.random.normal(jax.random.fold_in(_rk, 12), (4, 64), jnp.float32)
        return (x, fside_BxSxS_0, cond_512)
    x, fside_BxSxS_0, cond_512 = _rec_inputs()

    def _L0_cond_setup():
        import jax, jax.numpy as jnp
        from jax import lax
        import numpy as np
        B, T, C, TD = (8, 256, 256, 64)

        def _bi_wkv(r, k, v, w, u, time_emb):
            tf = jax.nn.sigmoid(jnp.sum(time_emb, axis=-1))[:, None, None]
            decay = jnp.exp(-jnp.exp(w.astype(jnp.float32)))[None, :] * (0.5 + 0.5 * tf[:, :, 0])
            kf = k.astype(jnp.float32)
            vf = v.astype(jnp.float32)
            ek = jnp.exp(jnp.minimum(kf, 30.0))
            ekv = ek * vf

            def step(carry, x):
                a, b = carry
                ekv_t, ek_t = x
                a = a * decay + ekv_t
                b = b * decay + ek_t
                return ((a, b), (a, b))
            ekv_t = jnp.swapaxes(ekv, 0, 1)
            ek_t = jnp.swapaxes(ek, 0, 1)
            init = (jnp.zeros_like(decay), jnp.zeros_like(decay))
            _, (nf, df) = lax.scan(step, init, (ekv_t, ek_t))
            _, (nb, db) = lax.scan(step, init, (ekv_t, ek_t), reverse=True)
            nf = jnp.swapaxes(nf, 0, 1)
            df = jnp.swapaxes(df, 0, 1)
            nb = jnp.swapaxes(nb, 0, 1)
            db = jnp.swapaxes(db, 0, 1)
            euk = jnp.exp(jnp.minimum(u.astype(jnp.float32)[None, None, :] + kf, 30.0))
            num = nf + nb - ekv + euk * vf
            den = df + db - ek + euk
            base = jax.nn.sigmoid(r.astype(jnp.float32)) * (num / jnp.maximum(den, 1e-08))
            out = base * (0.8 + 0.2 * tf)
            return out.astype(r.dtype)
        key = jax.random.key(seed)
        ks = jax.random.split(key, 6)
        return {'r': jax.random.normal(ks[0], (B, T, C), dtype=jnp.float32), 'k': jax.random.normal(ks[1], (B, T, C), dtype=jnp.float32), 'v': jax.random.normal(ks[2], (B, T, C), dtype=jnp.float32), 'w': jax.random.normal(ks[3], (C,), dtype=jnp.float32), 'u': jax.random.normal(ks[4], (C,), dtype=jnp.float32), 'time_emb': jax.random.normal(ks[5], (B, TD), dtype=jnp.float32)}
    _L0_cond_all = _L0_cond_setup()
    _L0_cond_in = {k: v for k, v in _L0_cond_all.items() if k in ('w', 'u')}
    del _L0_cond_all

    def _L0_attn_setup():
        import jax, jax.numpy as jnp
        import numpy as np
        NH = 16
        key = jax.random.key(seed)
        ks = jax.random.split(key, 5)
        B, T, D = (2, 256, 256)
        scale = 0.02
        return {'x': jax.random.normal(ks[0], (B, T, D), dtype=jnp.float32), 'Wq': jax.random.normal(ks[1], (D, D), dtype=jnp.float32) * scale, 'Wk': jax.random.normal(ks[2], (D, D), dtype=jnp.float32) * scale, 'Wv': jax.random.normal(ks[3], (D, D), dtype=jnp.float32) * scale, 'Wo': jax.random.normal(ks[4], (D, D), dtype=jnp.float32) * scale}
    _L0_attn_all = _L0_attn_setup()
    _L0_attn_in = {k: v for k, v in _L0_attn_all.items() if k in ('Wq', 'Wk', 'Wv', 'Wo')}
    del _L0_attn_all

    def _L0_cond2_setup():
        import jax, jax.numpy as jnp
        from jax import lax
        import numpy as np
        B, T, C, TD = (8, 256, 256, 64)

        def _bi_wkv(r, k, v, w, u, time_emb):
            tf = jax.nn.sigmoid(jnp.sum(time_emb, axis=-1))[:, None, None]
            decay = jnp.exp(-jnp.exp(w.astype(jnp.float32)))[None, :] * (0.5 + 0.5 * tf[:, :, 0])
            kf = k.astype(jnp.float32)
            vf = v.astype(jnp.float32)
            ek = jnp.exp(jnp.minimum(kf, 30.0))
            ekv = ek * vf

            def step(carry, x):
                a, b = carry
                ekv_t, ek_t = x
                a = a * decay + ekv_t
                b = b * decay + ek_t
                return ((a, b), (a, b))
            ekv_t = jnp.swapaxes(ekv, 0, 1)
            ek_t = jnp.swapaxes(ek, 0, 1)
            init = (jnp.zeros_like(decay), jnp.zeros_like(decay))
            _, (nf, df) = lax.scan(step, init, (ekv_t, ek_t))
            _, (nb, db) = lax.scan(step, init, (ekv_t, ek_t), reverse=True)
            nf = jnp.swapaxes(nf, 0, 1)
            df = jnp.swapaxes(df, 0, 1)
            nb = jnp.swapaxes(nb, 0, 1)
            db = jnp.swapaxes(db, 0, 1)
            euk = jnp.exp(jnp.minimum(u.astype(jnp.float32)[None, None, :] + kf, 30.0))
            num = nf + nb - ekv + euk * vf
            den = df + db - ek + euk
            base = jax.nn.sigmoid(r.astype(jnp.float32)) * (num / jnp.maximum(den, 1e-08))
            out = base * (0.8 + 0.2 * tf)
            return out.astype(r.dtype)
        key = jax.random.key(seed)
        ks = jax.random.split(key, 6)
        return {'r': jax.random.normal(ks[0], (B, T, C), dtype=jnp.float32), 'k': jax.random.normal(ks[1], (B, T, C), dtype=jnp.float32), 'v': jax.random.normal(ks[2], (B, T, C), dtype=jnp.float32), 'w': jax.random.normal(ks[3], (C,), dtype=jnp.float32), 'u': jax.random.normal(ks[4], (C,), dtype=jnp.float32), 'time_emb': jax.random.normal(ks[5], (B, TD), dtype=jnp.float32)}
    _L0_cond2_all = _L0_cond2_setup()
    _L0_cond2_in = {k: v for k, v in _L0_cond2_all.items() if k in ('w', 'u')}
    del _L0_cond2_all

    def _L0_ffn_setup():
        import jax, jax.numpy as jnp
        import numpy as np
        EPS = 1e-08

        def _rmsnorm(x, g):
            return g * (x * jax.lax.rsqrt(jnp.mean(x * x, axis=-1, keepdims=True) + EPS))

        def _act_quant(x):
            scale = 127.0 / jnp.clip(jnp.max(jnp.abs(x), axis=-1, keepdims=True), 0.0001, None)
            y = jnp.clip(jnp.round(x * scale), -128, 127) / scale
            return x + jax.lax.stop_gradient(y - x)

        def _ternary_quant(w):
            s = jnp.mean(jnp.abs(w))
            wq = jnp.round(jnp.tanh(w / (s + EPS))) * jnp.arctanh(s)
            return w + jax.lax.stop_gradient(wq - w)

        def _linear_bit(x, w, g):
            xq = _act_quant(_rmsnorm(x, g))
            wq = _ternary_quant(w)
            return jnp.einsum('bsd,od->bso', xq, wq)
        key = jax.random.key(seed)
        k = jax.random.split(key, 4)
        B, S, D, H = (4, 256, 256, 1024)
        std_up = float(np.sqrt(2.0 / (D + H)))
        std_dn = float(np.sqrt(2.0 / (H + D)))
        return {'x': jax.random.normal(k[0], (B, S, D), dtype=jnp.float32), 'w1': jax.random.normal(k[1], (H, D), dtype=jnp.float32) * std_up, 'g1': jnp.ones((D,), dtype=jnp.float32), 'w2': jax.random.normal(k[2], (H, D), dtype=jnp.float32) * std_up, 'g2': jnp.ones((D,), dtype=jnp.float32), 'w3': jax.random.normal(k[3], (D, H), dtype=jnp.float32) * std_dn, 'g3': jnp.ones((H,), dtype=jnp.float32)}
    _L0_ffn_all = _L0_ffn_setup()
    _L0_ffn_in = {k: v for k, v in _L0_ffn_all.items() if k in ('w1', 'g1', 'w2', 'g2', 'w3', 'g3')}
    del _L0_ffn_all

    def _L1_cond_setup():
        import jax, jax.numpy as jnp
        from jax import lax
        import numpy as np
        B, T, C, TD = (8, 256, 256, 64)

        def _bi_wkv(r, k, v, w, u, time_emb):
            tf = jax.nn.sigmoid(jnp.sum(time_emb, axis=-1))[:, None, None]
            decay = jnp.exp(-jnp.exp(w.astype(jnp.float32)))[None, :] * (0.5 + 0.5 * tf[:, :, 0])
            kf = k.astype(jnp.float32)
            vf = v.astype(jnp.float32)
            ek = jnp.exp(jnp.minimum(kf, 30.0))
            ekv = ek * vf

            def step(carry, x):
                a, b = carry
                ekv_t, ek_t = x
                a = a * decay + ekv_t
                b = b * decay + ek_t
                return ((a, b), (a, b))
            ekv_t = jnp.swapaxes(ekv, 0, 1)
            ek_t = jnp.swapaxes(ek, 0, 1)
            init = (jnp.zeros_like(decay), jnp.zeros_like(decay))
            _, (nf, df) = lax.scan(step, init, (ekv_t, ek_t))
            _, (nb, db) = lax.scan(step, init, (ekv_t, ek_t), reverse=True)
            nf = jnp.swapaxes(nf, 0, 1)
            df = jnp.swapaxes(df, 0, 1)
            nb = jnp.swapaxes(nb, 0, 1)
            db = jnp.swapaxes(db, 0, 1)
            euk = jnp.exp(jnp.minimum(u.astype(jnp.float32)[None, None, :] + kf, 30.0))
            num = nf + nb - ekv + euk * vf
            den = df + db - ek + euk
            base = jax.nn.sigmoid(r.astype(jnp.float32)) * (num / jnp.maximum(den, 1e-08))
            out = base * (0.8 + 0.2 * tf)
            return out.astype(r.dtype)
        key = jax.random.key(seed)
        ks = jax.random.split(key, 6)
        return {'r': jax.random.normal(ks[0], (B, T, C), dtype=jnp.float32), 'k': jax.random.normal(ks[1], (B, T, C), dtype=jnp.float32), 'v': jax.random.normal(ks[2], (B, T, C), dtype=jnp.float32), 'w': jax.random.normal(ks[3], (C,), dtype=jnp.float32), 'u': jax.random.normal(ks[4], (C,), dtype=jnp.float32), 'time_emb': jax.random.normal(ks[5], (B, TD), dtype=jnp.float32)}
    _L1_cond_all = _L1_cond_setup()
    _L1_cond_in = {k: v for k, v in _L1_cond_all.items() if k in ('w', 'u')}
    del _L1_cond_all

    def _L1_attn_setup():
        import jax, jax.numpy as jnp
        import numpy as np
        B_, L_, D_MODEL = (2, 256, 256)
        EXPAND = 2
        D_IN = EXPAND * D_MODEL
        HEADS = 64
        HEAD_DIM = D_IN // HEADS
        STATE = 128
        NGROUPS = 1
        K = 4
        CONV_DIM = D_IN + 2 * NGROUPS * STATE
        PROJ = D_IN + CONV_DIM + HEADS
        CHUNK = 32
        EPS = 1e-05

        def _segsum(x):
            T = x.shape[-1]
            c = jnp.cumsum(x, axis=-1)
            seg = c[..., :, None] - c[..., None, :]
            return jnp.where(jnp.tril(jnp.ones((T, T), bool)), seg, -jnp.inf)

        def _ssd(x, dA, Bm, Cm):
            b, l, h, p = x.shape
            n = Bm.shape[-1]
            c = l // CHUNK
            rep = h // Bm.shape[2]
            Bh = jnp.repeat(Bm, rep, axis=2).reshape(b, c, CHUNK, h, n)
            Ch = jnp.repeat(Cm, rep, axis=2).reshape(b, c, CHUNK, h, n)
            x = x.reshape(b, c, CHUNK, h, p)
            dA = dA.reshape(b, c, CHUNK, h).transpose(0, 3, 1, 2)
            dA_cum = jnp.cumsum(dA, axis=-1)
            Lmat = jnp.exp(_segsum(dA))
            Y_diag = jnp.einsum('bcthn,bcshn,bhcts,bcshp->bcthp', Ch, Bh, Lmat, x)
            decay_states = jnp.exp(dA_cum[..., -1:] - dA_cum)
            states = jnp.einsum('bcshn,bhcs,bcshp->bchpn', Bh, decay_states, x)
            chunk_decay = jnp.exp(_segsum(jnp.pad(dA_cum[..., -1], ((0, 0), (0, 0), (1, 0)))))
            states = jnp.concatenate([jnp.zeros_like(states[:, :1]), states], axis=1)
            prev = jnp.einsum('bhzc,bchpn->bzhpn', chunk_decay, states)[:, :-1]
            Y_off = jnp.einsum('bcthn,bchpn,bhct->bcthp', Ch, prev, jnp.exp(dA_cum))
            return (Y_diag + Y_off).reshape(b, l, h, p)
        key = jax.random.key(seed)
        ks = jax.random.split(key, 4)
        return {'hidden_states': jax.random.normal(ks[0], (B_, L_, D_MODEL), jnp.float32), 'in_proj_w': jax.random.normal(ks[1], (PROJ, D_MODEL), jnp.float32) * 0.02, 'conv_w': jax.random.normal(ks[2], (CONV_DIM, K), jnp.float32) * 0.2, 'conv_b': jnp.zeros((CONV_DIM,), jnp.float32), 'dt_bias': jnp.ones((HEADS,), jnp.float32), 'A_log': jnp.log(jnp.arange(1, HEADS + 1, dtype=jnp.float32)), 'D': jnp.ones((HEADS,), jnp.float32), 'norm_w': jnp.ones((D_IN,), jnp.float32), 'out_proj_w': jax.random.normal(ks[3], (D_MODEL, D_IN), jnp.float32) * 0.02}
    _L1_attn_all = _L1_attn_setup()
    _L1_attn_in = {k: v for k, v in _L1_attn_all.items() if k in ('in_proj_w', 'conv_w', 'conv_b', 'dt_bias', 'A_log', 'D', 'norm_w', 'out_proj_w')}
    del _L1_attn_all

    def _L1_cond2_setup():
        import jax, jax.numpy as jnp
        from jax import lax
        import numpy as np
        B, T, C, TD = (8, 256, 256, 64)

        def _bi_wkv(r, k, v, w, u, time_emb):
            tf = jax.nn.sigmoid(jnp.sum(time_emb, axis=-1))[:, None, None]
            decay = jnp.exp(-jnp.exp(w.astype(jnp.float32)))[None, :] * (0.5 + 0.5 * tf[:, :, 0])
            kf = k.astype(jnp.float32)
            vf = v.astype(jnp.float32)
            ek = jnp.exp(jnp.minimum(kf, 30.0))
            ekv = ek * vf

            def step(carry, x):
                a, b = carry
                ekv_t, ek_t = x
                a = a * decay + ekv_t
                b = b * decay + ek_t
                return ((a, b), (a, b))
            ekv_t = jnp.swapaxes(ekv, 0, 1)
            ek_t = jnp.swapaxes(ek, 0, 1)
            init = (jnp.zeros_like(decay), jnp.zeros_like(decay))
            _, (nf, df) = lax.scan(step, init, (ekv_t, ek_t))
            _, (nb, db) = lax.scan(step, init, (ekv_t, ek_t), reverse=True)
            nf = jnp.swapaxes(nf, 0, 1)
            df = jnp.swapaxes(df, 0, 1)
            nb = jnp.swapaxes(nb, 0, 1)
            db = jnp.swapaxes(db, 0, 1)
            euk = jnp.exp(jnp.minimum(u.astype(jnp.float32)[None, None, :] + kf, 30.0))
            num = nf + nb - ekv + euk * vf
            den = df + db - ek + euk
            base = jax.nn.sigmoid(r.astype(jnp.float32)) * (num / jnp.maximum(den, 1e-08))
            out = base * (0.8 + 0.2 * tf)
            return out.astype(r.dtype)
        key = jax.random.key(seed)
        ks = jax.random.split(key, 6)
        return {'r': jax.random.normal(ks[0], (B, T, C), dtype=jnp.float32), 'k': jax.random.normal(ks[1], (B, T, C), dtype=jnp.float32), 'v': jax.random.normal(ks[2], (B, T, C), dtype=jnp.float32), 'w': jax.random.normal(ks[3], (C,), dtype=jnp.float32), 'u': jax.random.normal(ks[4], (C,), dtype=jnp.float32), 'time_emb': jax.random.normal(ks[5], (B, TD), dtype=jnp.float32)}
    _L1_cond2_all = _L1_cond2_setup()
    _L1_cond2_in = {k: v for k, v in _L1_cond2_all.items() if k in ('w', 'u')}
    del _L1_cond2_all

    def _L1_ffn_setup():
        import jax, jax.numpy as jnp
        import numpy as np
        NUM_EXPERTS = 8
        TOP_K = 2
        HIDDEN = 256
        FFN = 704
        BATCH, SEQ = (2, 128)
        key = jax.random.key(seed)
        ks = jax.random.split(key, 5)
        scale = 0.02
        hidden_states = jax.random.normal(ks[0], (BATCH, SEQ, HIDDEN), dtype=jnp.float32)
        w_gate = jax.random.normal(ks[1], (NUM_EXPERTS, HIDDEN), dtype=jnp.float32) * scale
        w1 = jax.random.normal(ks[2], (NUM_EXPERTS, FFN, HIDDEN), dtype=jnp.float32) * scale
        w2 = jax.random.normal(ks[3], (NUM_EXPERTS, HIDDEN, FFN), dtype=jnp.float32) * scale
        w3 = jax.random.normal(ks[4], (NUM_EXPERTS, FFN, HIDDEN), dtype=jnp.float32) * scale
        return {'hidden_states': hidden_states, 'w_gate': w_gate, 'w1': w1, 'w2': w2, 'w3': w3}
    _L1_ffn_all = _L1_ffn_setup()
    _L1_ffn_in = {k: v for k, v in _L1_ffn_all.items() if k in ('w_gate', 'w1', 'w2', 'w3')}
    del _L1_ffn_all
    return {'x': x, 'fside_BxSxS_0': fside_BxSxS_0, 'cond_512': cond_512, 'L0_cond_w': _L0_cond_in['w'], 'L0_cond_u': _L0_cond_in['u'], 'L0_attn_Wq': _L0_attn_in['Wq'], 'L0_attn_Wk': _L0_attn_in['Wk'], 'L0_attn_Wv': _L0_attn_in['Wv'], 'L0_attn_Wo': _L0_attn_in['Wo'], 'L0_cond2_w': _L0_cond2_in['w'], 'L0_cond2_u': _L0_cond2_in['u'], 'L0_ffn_w1': _L0_ffn_in['w1'], 'L0_ffn_g1': _L0_ffn_in['g1'], 'L0_ffn_w2': _L0_ffn_in['w2'], 'L0_ffn_g2': _L0_ffn_in['g2'], 'L0_ffn_w3': _L0_ffn_in['w3'], 'L0_ffn_g3': _L0_ffn_in['g3'], 'L1_cond_w': _L1_cond_in['w'], 'L1_cond_u': _L1_cond_in['u'], 'L1_attn_in_proj_w': _L1_attn_in['in_proj_w'], 'L1_attn_conv_w': _L1_attn_in['conv_w'], 'L1_attn_conv_b': _L1_attn_in['conv_b'], 'L1_attn_dt_bias': _L1_attn_in['dt_bias'], 'L1_attn_A_log': _L1_attn_in['A_log'], 'L1_attn_D': _L1_attn_in['D'], 'L1_attn_norm_w': _L1_attn_in['norm_w'], 'L1_attn_out_proj_w': _L1_attn_in['out_proj_w'], 'L1_cond2_w': _L1_cond2_in['w'], 'L1_cond2_u': _L1_cond2_in['u'], 'L1_ffn_w_gate': _L1_ffn_in['w_gate'], 'L1_ffn_w1': _L1_ffn_in['w1'], 'L1_ffn_w2': _L1_ffn_in['w2'], 'L1_ffn_w3': _L1_ffn_in['w3']}

def reference(x, fside_BxSxS_0, cond_512, L0_cond_w, L0_cond_u, L0_attn_Wq, L0_attn_Wk, L0_attn_Wv, L0_attn_Wo, L0_cond2_w, L0_cond2_u, L0_ffn_w1, L0_ffn_g1, L0_ffn_w2, L0_ffn_g2, L0_ffn_w3, L0_ffn_g3, L1_cond_w, L1_cond_u, L1_attn_in_proj_w, L1_attn_conv_w, L1_attn_conv_b, L1_attn_dt_bias, L1_attn_A_log, L1_attn_D, L1_attn_norm_w, L1_attn_out_proj_w, L1_cond2_w, L1_cond2_u, L1_ffn_w_gate, L1_ffn_w1, L1_ffn_w2, L1_ffn_w3):
    import jax
    import jax.numpy as jnp

    def _L0_cond_ref(r, k, v, w, u, time_emb):
        import jax, jax.numpy as jnp
        from jax import lax
        import numpy as np
        B, T, C, TD = (8, 256, 256, 64)

        def _bi_wkv(r, k, v, w, u, time_emb):
            tf = jax.nn.sigmoid(jnp.sum(time_emb, axis=-1))[:, None, None]
            decay = jnp.exp(-jnp.exp(w.astype(jnp.float32)))[None, :] * (0.5 + 0.5 * tf[:, :, 0])
            kf = k.astype(jnp.float32)
            vf = v.astype(jnp.float32)
            ek = jnp.exp(jnp.minimum(kf, 30.0))
            ekv = ek * vf

            def step(carry, x):
                a, b = carry
                ekv_t, ek_t = x
                a = a * decay + ekv_t
                b = b * decay + ek_t
                return ((a, b), (a, b))
            ekv_t = jnp.swapaxes(ekv, 0, 1)
            ek_t = jnp.swapaxes(ek, 0, 1)
            init = (jnp.zeros_like(decay), jnp.zeros_like(decay))
            _, (nf, df) = lax.scan(step, init, (ekv_t, ek_t))
            _, (nb, db) = lax.scan(step, init, (ekv_t, ek_t), reverse=True)
            nf = jnp.swapaxes(nf, 0, 1)
            df = jnp.swapaxes(df, 0, 1)
            nb = jnp.swapaxes(nb, 0, 1)
            db = jnp.swapaxes(db, 0, 1)
            euk = jnp.exp(jnp.minimum(u.astype(jnp.float32)[None, None, :] + kf, 30.0))
            num = nf + nb - ekv + euk * vf
            den = df + db - ek + euk
            base = jax.nn.sigmoid(r.astype(jnp.float32)) * (num / jnp.maximum(den, 1e-08))
            out = base * (0.8 + 0.2 * tf)
            return out.astype(r.dtype)
        return _bi_wkv(r, k, v, w, u, time_emb)

    def _L0_attn_ref(x, Wq, Wk, Wv, Wo):
        import jax, jax.numpy as jnp
        import numpy as np
        NH = 16
        B, T, D = x.shape
        hd = D // NH
        q = (x @ Wq.T).reshape(B, T, NH, hd).transpose(0, 2, 1, 3)
        k = (x @ Wk.T).reshape(B, T, NH, hd).transpose(0, 2, 1, 3)
        v = (x @ Wv.T).reshape(B, T, NH, hd).transpose(0, 2, 1, 3)
        att = jnp.einsum('bhtd,bhsd->bhts', q, k) / jnp.sqrt(jnp.asarray(hd, x.dtype))
        neg = jnp.finfo(att.dtype).min
        mask = jnp.triu(jnp.full((T, T), neg, dtype=att.dtype), k=1)
        att = att + mask
        w = jax.nn.softmax(att, axis=-1)
        z = jnp.einsum('bhts,bhsd->bhtd', w, v)
        z = z.transpose(0, 2, 1, 3).reshape(B, T, D)
        return z @ Wo.T

    def _L0_cond2_ref(r, k, v, w, u, time_emb):
        import jax, jax.numpy as jnp
        from jax import lax
        import numpy as np
        B, T, C, TD = (8, 256, 256, 64)

        def _bi_wkv(r, k, v, w, u, time_emb):
            tf = jax.nn.sigmoid(jnp.sum(time_emb, axis=-1))[:, None, None]
            decay = jnp.exp(-jnp.exp(w.astype(jnp.float32)))[None, :] * (0.5 + 0.5 * tf[:, :, 0])
            kf = k.astype(jnp.float32)
            vf = v.astype(jnp.float32)
            ek = jnp.exp(jnp.minimum(kf, 30.0))
            ekv = ek * vf

            def step(carry, x):
                a, b = carry
                ekv_t, ek_t = x
                a = a * decay + ekv_t
                b = b * decay + ek_t
                return ((a, b), (a, b))
            ekv_t = jnp.swapaxes(ekv, 0, 1)
            ek_t = jnp.swapaxes(ek, 0, 1)
            init = (jnp.zeros_like(decay), jnp.zeros_like(decay))
            _, (nf, df) = lax.scan(step, init, (ekv_t, ek_t))
            _, (nb, db) = lax.scan(step, init, (ekv_t, ek_t), reverse=True)
            nf = jnp.swapaxes(nf, 0, 1)
            df = jnp.swapaxes(df, 0, 1)
            nb = jnp.swapaxes(nb, 0, 1)
            db = jnp.swapaxes(db, 0, 1)
            euk = jnp.exp(jnp.minimum(u.astype(jnp.float32)[None, None, :] + kf, 30.0))
            num = nf + nb - ekv + euk * vf
            den = df + db - ek + euk
            base = jax.nn.sigmoid(r.astype(jnp.float32)) * (num / jnp.maximum(den, 1e-08))
            out = base * (0.8 + 0.2 * tf)
            return out.astype(r.dtype)
        return _bi_wkv(r, k, v, w, u, time_emb)

    def _L0_ffn_ref(x, w1, g1, w2, g2, w3, g3):
        import jax, jax.numpy as jnp
        import numpy as np
        EPS = 1e-08

        def _rmsnorm(x, g):
            return g * (x * jax.lax.rsqrt(jnp.mean(x * x, axis=-1, keepdims=True) + EPS))

        def _act_quant(x):
            scale = 127.0 / jnp.clip(jnp.max(jnp.abs(x), axis=-1, keepdims=True), 0.0001, None)
            y = jnp.clip(jnp.round(x * scale), -128, 127) / scale
            return x + jax.lax.stop_gradient(y - x)

        def _ternary_quant(w):
            s = jnp.mean(jnp.abs(w))
            wq = jnp.round(jnp.tanh(w / (s + EPS))) * jnp.arctanh(s)
            return w + jax.lax.stop_gradient(wq - w)

        def _linear_bit(x, w, g):
            xq = _act_quant(_rmsnorm(x, g))
            wq = _ternary_quant(w)
            return jnp.einsum('bsd,od->bso', xq, wq)
        swish = jax.nn.silu(_linear_bit(x, w1, g1))
        x_v = _linear_bit(x, w2, g2)
        h = swish * x_v
        return _linear_bit(h, w3, g3)

    def _L1_cond_ref(r, k, v, w, u, time_emb):
        import jax, jax.numpy as jnp
        from jax import lax
        import numpy as np
        B, T, C, TD = (8, 256, 256, 64)

        def _bi_wkv(r, k, v, w, u, time_emb):
            tf = jax.nn.sigmoid(jnp.sum(time_emb, axis=-1))[:, None, None]
            decay = jnp.exp(-jnp.exp(w.astype(jnp.float32)))[None, :] * (0.5 + 0.5 * tf[:, :, 0])
            kf = k.astype(jnp.float32)
            vf = v.astype(jnp.float32)
            ek = jnp.exp(jnp.minimum(kf, 30.0))
            ekv = ek * vf

            def step(carry, x):
                a, b = carry
                ekv_t, ek_t = x
                a = a * decay + ekv_t
                b = b * decay + ek_t
                return ((a, b), (a, b))
            ekv_t = jnp.swapaxes(ekv, 0, 1)
            ek_t = jnp.swapaxes(ek, 0, 1)
            init = (jnp.zeros_like(decay), jnp.zeros_like(decay))
            _, (nf, df) = lax.scan(step, init, (ekv_t, ek_t))
            _, (nb, db) = lax.scan(step, init, (ekv_t, ek_t), reverse=True)
            nf = jnp.swapaxes(nf, 0, 1)
            df = jnp.swapaxes(df, 0, 1)
            nb = jnp.swapaxes(nb, 0, 1)
            db = jnp.swapaxes(db, 0, 1)
            euk = jnp.exp(jnp.minimum(u.astype(jnp.float32)[None, None, :] + kf, 30.0))
            num = nf + nb - ekv + euk * vf
            den = df + db - ek + euk
            base = jax.nn.sigmoid(r.astype(jnp.float32)) * (num / jnp.maximum(den, 1e-08))
            out = base * (0.8 + 0.2 * tf)
            return out.astype(r.dtype)
        return _bi_wkv(r, k, v, w, u, time_emb)

    def _L1_attn_ref(hidden_states, in_proj_w, conv_w, conv_b, dt_bias, A_log, D, norm_w, out_proj_w):
        import jax, jax.numpy as jnp
        import numpy as np
        B_, L_, D_MODEL = (2, 256, 256)
        EXPAND = 2
        D_IN = EXPAND * D_MODEL
        HEADS = 64
        HEAD_DIM = D_IN // HEADS
        STATE = 128
        NGROUPS = 1
        K = 4
        CONV_DIM = D_IN + 2 * NGROUPS * STATE
        PROJ = D_IN + CONV_DIM + HEADS
        CHUNK = 32
        EPS = 1e-05

        def _segsum(x):
            T = x.shape[-1]
            c = jnp.cumsum(x, axis=-1)
            seg = c[..., :, None] - c[..., None, :]
            return jnp.where(jnp.tril(jnp.ones((T, T), bool)), seg, -jnp.inf)

        def _ssd(x, dA, Bm, Cm):
            b, l, h, p = x.shape
            n = Bm.shape[-1]
            c = l // CHUNK
            rep = h // Bm.shape[2]
            Bh = jnp.repeat(Bm, rep, axis=2).reshape(b, c, CHUNK, h, n)
            Ch = jnp.repeat(Cm, rep, axis=2).reshape(b, c, CHUNK, h, n)
            x = x.reshape(b, c, CHUNK, h, p)
            dA = dA.reshape(b, c, CHUNK, h).transpose(0, 3, 1, 2)
            dA_cum = jnp.cumsum(dA, axis=-1)
            Lmat = jnp.exp(_segsum(dA))
            Y_diag = jnp.einsum('bcthn,bcshn,bhcts,bcshp->bcthp', Ch, Bh, Lmat, x)
            decay_states = jnp.exp(dA_cum[..., -1:] - dA_cum)
            states = jnp.einsum('bcshn,bhcs,bcshp->bchpn', Bh, decay_states, x)
            chunk_decay = jnp.exp(_segsum(jnp.pad(dA_cum[..., -1], ((0, 0), (0, 0), (1, 0)))))
            states = jnp.concatenate([jnp.zeros_like(states[:, :1]), states], axis=1)
            prev = jnp.einsum('bhzc,bchpn->bzhpn', chunk_decay, states)[:, :-1]
            Y_off = jnp.einsum('bcthn,bchpn,bhct->bcthp', Ch, prev, jnp.exp(dA_cum))
            return (Y_diag + Y_off).reshape(b, l, h, p)
        b, l, _ = hidden_states.shape
        proj = hidden_states @ in_proj_w.T
        gate = proj[..., :D_IN]
        xBC = proj[..., D_IN:D_IN + CONV_DIM]
        dt = proj[..., D_IN + CONV_DIM:]
        xp = jnp.pad(xBC, ((0, 0), (K - 1, 0), (0, 0)))
        conv = conv_b + sum((conv_w[:, i] * xp[:, i:i + l, :] for i in range(K)))
        xBC = jax.nn.silu(conv)
        x = xBC[..., :D_IN].reshape(b, l, HEADS, HEAD_DIM)
        Bm = xBC[..., D_IN:D_IN + NGROUPS * STATE].reshape(b, l, NGROUPS, STATE)
        Cm = xBC[..., D_IN + NGROUPS * STATE:].reshape(b, l, NGROUPS, STATE)
        dt = jax.nn.softplus(dt + dt_bias)
        A = -jnp.exp(A_log)
        y = _ssd(x * dt[..., None], dt * A, Bm, Cm)
        y = y + D[None, None, :, None] * x
        y = y.reshape(b, l, D_IN)
        hg = y * jax.nn.silu(gate)
        var = jnp.mean(hg * hg, axis=-1, keepdims=True)
        y = hg * jax.lax.rsqrt(var + EPS) * norm_w
        return y @ out_proj_w.T

    def _L1_cond2_ref(r, k, v, w, u, time_emb):
        import jax, jax.numpy as jnp
        from jax import lax
        import numpy as np
        B, T, C, TD = (8, 256, 256, 64)

        def _bi_wkv(r, k, v, w, u, time_emb):
            tf = jax.nn.sigmoid(jnp.sum(time_emb, axis=-1))[:, None, None]
            decay = jnp.exp(-jnp.exp(w.astype(jnp.float32)))[None, :] * (0.5 + 0.5 * tf[:, :, 0])
            kf = k.astype(jnp.float32)
            vf = v.astype(jnp.float32)
            ek = jnp.exp(jnp.minimum(kf, 30.0))
            ekv = ek * vf

            def step(carry, x):
                a, b = carry
                ekv_t, ek_t = x
                a = a * decay + ekv_t
                b = b * decay + ek_t
                return ((a, b), (a, b))
            ekv_t = jnp.swapaxes(ekv, 0, 1)
            ek_t = jnp.swapaxes(ek, 0, 1)
            init = (jnp.zeros_like(decay), jnp.zeros_like(decay))
            _, (nf, df) = lax.scan(step, init, (ekv_t, ek_t))
            _, (nb, db) = lax.scan(step, init, (ekv_t, ek_t), reverse=True)
            nf = jnp.swapaxes(nf, 0, 1)
            df = jnp.swapaxes(df, 0, 1)
            nb = jnp.swapaxes(nb, 0, 1)
            db = jnp.swapaxes(db, 0, 1)
            euk = jnp.exp(jnp.minimum(u.astype(jnp.float32)[None, None, :] + kf, 30.0))
            num = nf + nb - ekv + euk * vf
            den = df + db - ek + euk
            base = jax.nn.sigmoid(r.astype(jnp.float32)) * (num / jnp.maximum(den, 1e-08))
            out = base * (0.8 + 0.2 * tf)
            return out.astype(r.dtype)
        return _bi_wkv(r, k, v, w, u, time_emb)

    def _L1_ffn_ref(hidden_states, w_gate, w1, w2, w3):
        import jax, jax.numpy as jnp
        import numpy as np
        NUM_EXPERTS = 8
        TOP_K = 2
        HIDDEN = 256
        FFN = 704
        BATCH, SEQ = (2, 128)
        B, S, D = hidden_states.shape
        x = hidden_states.reshape(-1, D)
        router_logits = x @ w_gate.T
        routing_weights = jax.nn.softmax(router_logits.astype(jnp.float32), axis=-1)
        routing_weights, selected_experts = jax.lax.top_k(routing_weights, TOP_K)
        routing_weights = routing_weights / jnp.sum(routing_weights, axis=-1, keepdims=True)
        routing_weights = routing_weights.astype(x.dtype)
        out = jnp.zeros_like(x)
        for e in range(NUM_EXPERTS):
            expert_weight = jnp.sum(routing_weights * (selected_experts == e), axis=-1, keepdims=True)
            h = jax.nn.silu(x @ w1[e].T) * (x @ w3[e].T)
            out = out + h @ w2[e].T * expert_weight
        return out.reshape(B, S, D)
    x = x + _L0_attn_ref(_L0_cond_ref(x, fside_BxSxS_0, fside_BxSxS_0, L0_cond_w, L0_cond_u, cond_512), L0_attn_Wq, L0_attn_Wk, L0_attn_Wv, L0_attn_Wo)
    x = x + _L0_ffn_ref(_L0_cond2_ref(x, fside_BxSxS_0, fside_BxSxS_0, L0_cond2_w, L0_cond2_u, cond_512), L0_ffn_w1, L0_ffn_g1, L0_ffn_w2, L0_ffn_g2, L0_ffn_w3, L0_ffn_g3)
    x = x + _L1_attn_ref(_L1_cond_ref(x, fside_BxSxS_0, fside_BxSxS_0, L1_cond_w, L1_cond_u, cond_512), L1_attn_in_proj_w, L1_attn_conv_w, L1_attn_conv_b, L1_attn_dt_bias, L1_attn_A_log, L1_attn_D, L1_attn_norm_w, L1_attn_out_proj_w)
    x = x + _L1_ffn_ref(_L1_cond2_ref(x, fside_BxSxS_0, fside_BxSxS_0, L1_cond2_w, L1_cond2_u, cond_512), L1_ffn_w_gate, L1_ffn_w1, L1_ffn_w2, L1_ffn_w3)
    return x

_drawn_inputs = setup_inputs


def setup_inputs(seed=0):
    import zlib

    import numpy as np

    out = dict(_drawn_inputs(seed))
    spreads = {'L0_ffn_g1': (1.0, 0.2),
     'L0_ffn_g2': (1.0, 0.2),
     'L0_ffn_g3': (1.0, 0.2),
     'L1_attn_conv_b': (0.0, 0.1),
     'L1_attn_dt_bias': (1.0, 0.6),
     'L1_attn_D': (1.0, 0.2),
     'L1_attn_norm_w': (1.0, 0.2)}
    factors = {'L0_cond_w': 3.511,
     'L0_cond_u': 5.887,
     'L0_attn_Wq': 8.0,
     'L0_attn_Wk': 8.0,
     'L1_attn_A_log': 8.0,
     'L1_cond2_w': 8.0,
     'L1_cond2_u': 8.0,
     'L1_ffn_w_gate': 8.0,
     'L1_ffn_w1': 8.0,
     'L1_ffn_w2': 8.0,
     'L1_ffn_w3': 8.0}
    for name, (base, spread) in spreads.items():
        noise = np.random.default_rng([zlib.crc32(name.encode()), seed]).standard_normal(out[name].shape)
        drawn = base * np.exp(spread * noise) if base else spread * noise
        out[name] = jnp.asarray(drawn.astype(out[name].dtype))
    for name, factor in factors.items():
        out[name] = (out[name] * factor).astype(out[name].dtype)
    return out
```

```python
import concourse.bass as bass
from concourse import mybir
from contextlib import ExitStack

P = 128
B, T, D = 4, 256, 256
N = B * T
CT = D // P
NT = N // P
HALF = 512
NCH = N // HALF
NH, HD = 16, 16
G4 = NH // 4
H = 1024
HT = H // P
DIN, NS, SH, SP_ = 512, 128, 64, 8
XT = DIN // P
Q = 32
NC = P // Q
HG = SH // 4
PROJ = DIN + DIN + 2 * NS + SH
NE, FF = 8, 704
MT = NE * FF // P
RING = 6
MAGIC = 1.5 * 2.0 ** 23


def build(nc, a, out):
    F = mybir.dt.float32
    BF = mybir.dt.bfloat16
    U32 = mybir.dt.uint32
    ALU = mybir.AluOpType
    ACT = mybir.ActivationFunctionType
    X = mybir.AxisListType.X

    with ExitStack() as ctx:
        def sb(name, shape, dt=F):
            return ctx.enter_context(nc.sbuf_tensor(name, shape, dt))

        def sem(name):
            return ctx.enter_context(nc.semaphore(name))

        ARENA = 30 * 1024
        arena = sb("arena", [P, ARENA])
        K = 1024

        xT = sb("xT", [P, CT, N])
        A = sb("A", [P, CT, N])
        R = sb("R", [P, 4, CT, N])
        ident = sb("ident", [P, P])
        identb = sb("identb", [P, P], BF)
        ones = sb("ones", [P, P])
        negmask = sb("negmask", [P, P], BF)
        negmaskf = arena[:, 26 * K:26 * K + P]
        ugt = sb("ugt", [P, P])
        tri = sb("tri", [P, P])
        cones = sb("cones", [P, NC, P])
        step = sb("step", [P, Q])
        hmask = sb("hmask", [P, 8])
        iota = sb("iota", [P, NE])
        condT = sb("condT", [64, B])
        wu = sb("wu", [P, 4, 2, CT])
        inproj = sb("inproj", [P, CT, PROJ])
        outproj = sb("outproj", [P, XT, D])
        convw = sb("convw", [P, 6, 4])
        convb = sb("convb", [P, 6])
        dtb = sb("dtb", [P, SH])
        alog = sb("alog", [P, SH])
        alogj = sb("alogj", [P, HG])
        dskip = sb("dskip", [P, XT])
        normw = sb("normw", [P, XT])
        wgate = sb("wgate", [P, CT, NE])
        tf = sb("tf", [P, B])
        hf = sb("hf", [P, B])
        cb = sb("cb", [P, B])
        ew = sb("ewx", [P, 4, CT])
        dec = sb("dec", [P, 4, CT, B])
        wabs = sb("wabs", [P, 3])
        wsc = sb("wsc", [P, 3])
        winv = sb("winv", [P, 3])
        wat = sb("wat", [P, 3])
        wtmp = sb("wtmp", [P, 3])
        small = sb("small", [P, 16, NT])

        fT = arena[:, 0:2 * K].rearrange("p (a n) -> p a n", a=CT)
        ek = arena[:, 2 * K:4 * K].rearrange("p (a n) -> p a n", a=CT)
        ekv = arena[:, 4 * K:6 * K].rearrange("p (a n) -> p a n", a=CT)
        euk = [arena[:, (6 + i) * K:(7 + i) * K] for i in range(2)]
        nf, nb, df, db, gg, gf = (arena[:, (8 + i) * K:(9 + i) * K] for i in range(6))
        wraw = arena[:, 14 * K:20 * K].rearrange("p (w n) -> p w n", w=3)
        wter = arena[:, 27 * K:30 * K].bitcast(BF).rearrange("p (w n) -> p w n", w=3)
        gb = sb("gb", [P, 2 * D + H])
        wqkvo = arena[:, 20 * K:22 * K].rearrange("p (w k n) -> p w k n", w=4, k=CT)
        qT = arena[:, 0:2 * K].rearrange("p (a n) -> p a n", a=CT)
        kT = arena[:, 2 * K:4 * K].rearrange("p (a n) -> p a n", a=CT)
        qm = [arena[:, 4 * K + 512 * i:4 * K + 512 * (i + 1)].rearrange("p (j t) -> p j t", j=4) for i in range(2)]
        vv = arena[:, 8 * K:10 * K].rearrange("p (i n) -> p i n", i=NT)
        pr = [arena[:, (10 + i) * K:(11 + i) * K].rearrange("p (j s) -> p j s", j=4) for i in range(2)]
        pt = [arena[:, (12 + i) * K:(13 + i) * K] for i in range(2)]
        zT = arena[:, 14 * K:16 * K].rearrange("p (a n) -> p a n", a=CT)
        zn = [arena[:, 16 * K + 256 * i:16 * K + 256 * (i + 1)] for i in range(2)]
        nmx = sb("nmx", [P, 2, 4])
        rsum = sb("rsum", [P, 2, NH])
        rinv = sb("rinv", [P, 2, NH])
        atok = arena[:, 0:2 * K].rearrange("p (i n) -> p i n", i=NT)
        yy = arena[:, 2 * K:4 * K].rearrange("p (i n) -> p i n", i=NT)
        yq = arena[:, 4 * K:6 * K].rearrange("p (i n) -> p i n", i=NT)
        xqb = arena[:, 6 * K:7 * K].bitcast(BF).rearrange("p (i n) -> p i n", i=NT)
        xqT = [arena[:, (7 + i) * K:(8 + i) * K].bitcast(BF).rearrange("p (a n) -> p a n", a=CT) for i in range(2)]
        hh = arena[:, 9 * K:17 * K].rearrange("p (i n) -> p i n", i=NT)
        sw = [arena[:, (17 + i) * K:(18 + i) * K] for i in range(2)]
        y3 = [arena[:, (19 + i) * K:(20 + i) * K] for i in range(2)]
        hq = [arena[:, 21 * K + 512 * i:21 * K + 512 * (i + 1)].bitcast(BF) for i in range(2)]
        hqT = [arena[:, 22 * K + 512 * i:22 * K + 512 * (i + 1)].bitcast(BF).rearrange("p (k n) -> p k n", k=HT) for i in range(2)]
        otok = [arena[:, 23 * K + 256 * i:23 * K + 256 * (i + 1)] for i in range(2)]
        sg = arena[:, 0:4 * K].rearrange("p (a n) -> p a n", a=XT)
        xc = arena[:, 4 * K:10 * K].rearrange("p (a n) -> p a n", a=6)
        ya = arena[:, 10 * K:14 * K].rearrange("p (a n) -> p a n", a=XT)
        cd = arena[:, 14 * K:16 * K].rearrange("p (c i h) -> p c i h", c=NC, i=NT)
        stp = arena[:, 16 * K:18 * K].rearrange("p (c h t) -> p c h t", c=NC, h=HG)
        lm = arena[:, 18 * K:20 * K].rearrange("p (c h t) -> p c h t", c=NC, h=HG)
        xbd = arena[:, 20 * K:22 * K].rearrange("p (c h j q) -> p c h j q", c=NC, h=HG, j=4)
        dt = arena[:, 22 * K:22 * K + 512].rearrange("p (i h) -> p i h", i=NT)
        dA = arena[:, 22 * K + 512:23 * K].rearrange("p (i h) -> p i h", i=NT)
        dtj = arena[:, 23 * K:23 * K + 512].rearrange("p (i c h) -> p i c h", i=NT, c=NC)
        dAj = arena[:, 23 * K + 512:24 * K].rearrange("p (i c h) -> p i c h", i=NT, c=NC)
        ddt = arena[:, 24 * K:24 * K + 512].rearrange("p (i h) -> p i h", i=NT)
        t1 = arena[:, 24 * K + 512:25 * K]
        gm = arena[:, 25 * K:25 * K + 128].rearrange("p (c t) -> p c t", c=NC)
        btok = arena[:, 25 * K + 128:25 * K + 256]
        xdd = arena[:, 25 * K + 512:26 * K]
        dAe = arena[:, 29 * K:29 * K + 512]
        es = arena[:, 26 * K:26 * K + 512]
        yo = arena[:, 26 * K + 512:27 * K]
        st = [arena[:, 27 * K + 512 * i:27 * K + 512 * (i + 1)] for i in range(2)]
        rs = arena[:, 28 * K:29 * K]
        anegb = sb("anegb", [P, SH])
        anegj = sb("anegj", [P, HG])
        ewb = arena[:, 0:8 * K].rearrange("p (e n) -> p e n", e=NE)
        ring = arena[:, 8 * K:8 * K + RING * 768].rearrange("p (r n) -> p r n", r=RING)
        hs = [arena[:, 14 * K + 512 * i:14 * K + 512 * (i + 1)] for i in range(2)]
        hw = [arena[:, 15 * K + 512 * i:15 * K + 512 * (i + 1)] for i in range(4)]
        sele = arena[0:NE, 18 * K:19 * K].rearrange("e (f n) -> e f n", f=NE)
        lg = sb("lg", [P, NT, NE])
        pe8 = sb("pe8", [P, NT, NE])
        top = sb("top", [P, NT, NE])
        tix = sb("tix", [P, NT, NE], U32)
        tixf = sb("tixf", [P, NT, NE])
        ewt = sb("ewt", [P, NT, NE])
        ewm = sb("ewm", [P, NT, NE])
        ewT = arena[0:NE, 17 * K:18 * K]
        mx8 = sb("mx8", [P, NT])

        PS = ctx.enter_context(nc.psum_tensor("PS", [P, 8, HALF], F))
        PSB = PS[:, :, :].rearrange("p b n -> p (b n)")

        def bank(i, n=HALF):
            return PS[:, i, 0:n]

        ld = {k: sem("ld_" + k) for k in ("x", "f", "const", "small", "ffn", "attn", "ssd", "sele")}
        ld_ring = [sem(f"ld_ring{i}") for i in range(RING)]
        st_out = sem("st_out")
        NAMES = """pool_qm dve_self act_self pool_self pe_cond act_cond dve_uk act_euk act_ek dve_wabs pe_wsum dve_winv
            act_tanh dve_tern act_exw act_atanh dve_ln
            act_sg dve_A pe_q pe_k pe_v act_q dve_k dve_v pe_sc dve_max act_exp pe_pt act_pt pe_z dve_zn pe_zt act_zt pe_wo dve_x
            pe_at dve_atok act_ss dve_var act_sqrt dve_xq pe_xqt act_xqt pe_h act_sw dve_h act_ss3 dve_hq pe_hqt act_hqt pe_o act_o pe_ot
            pe_gate act_gate pe_xbc act_cv dve_cv act_xc pe_dt dve_dtx act_sp1 act_sp2 dve_dt pe_dec act_dec act_cd dve_ddt
            pe_tok dve_xbd dve_tok pool_stp pool_dae pe_seg act_seg dve_gm dve_m pe_e act_e pe_yd pe_yo dve_y pe_sl dve_s
            dve_hg act_hg2 act_hgw pe_var dve_v2 act_sq2 dve_rs pe_op
            pe_lg dve_lg act_pe dve_ew pe_ewt act_ewt pe_ewb act_ewb pe_up act_hs dve_hw pe_dn dve_out""".split()
        S = {n: sem(n) for n in NAMES}

        def chained(eng, own):
            count = {}

            def done(ins, name=own):
                count[name] = count.get(name, 0) + 1
                ins.then_inc(S[name], 1)
                eng.wait_ge(S[name], count[name])
            return done

        block = ctx.enter_context(nc.Block())

        @block.sync
        def _(sp):
            def load(dst, src, group):
                sp.dma_start(dst, src).then_inc(ld[group], 16)

            load(fT, a["fT"], "f")
            load(wu[:], a["wu"], "small")
            load(condT[:], a["condT"], "small")
            load(ones[:], a["ones"], "small")
            load(xT[:], a["xT"], "x")
            load(wraw[:, 0, :], a["w1T"], "ffn")
            load(wraw[:, 1, :], a["w2T"], "ffn")
            load(wraw[:, 2, :], a["w3T"], "ffn")
            load(gb[:], a["gb"], "ffn")
            for n, m in (("ident", ident), ("negmask", negmaskf), ("ugt", ugt), ("tri", tri),
                         ("cones", cones), ("step", step), ("iota", iota)):
                load(m[:], a[n], "const")
            load(wqkvo, a["wqkvo"], "attn")
            load(hmask[:], a["hmask"], "attn")
            for n, m in (("inproj", inproj), ("outproj", outproj), ("convw", convw), ("convb", convb), ("dtb", dtb),
                         ("alog", alog), ("alogj", alogj), ("dskip", dskip), ("normw", normw), ("wgate", wgate)):
                load(m[:], a[n], "ssd")
            sp.wait_ge(S["dve_x"], X_SSD)
            load(sele, a["sele"], "sele")
            for i in range(MT):
                if i >= RING:
                    sp.wait_ge(S["pe_dn"], i - RING + 1)
                sp.dma_start(ring[:, i % RING, :], a["moe"][i]).then_inc(ld_ring[i % RING], 16)
            sp.wait_ge(S["dve_out"], 4)
            sp.dma_start(out, xT[:]).then_inc(st_out, 16)
            sp.wait_ge(st_out, 16)

        @block.gpsimd
        def _(pool):
            pool.wait_ge(ld["attn"], 32)
            pool.wait_ge(S["act_q"], 4)
            for u in range(32):
                i, g = divmod(u, 4)
                if u >= 2:
                    pool.wait_ge(S["pe_sc"], u - 1)
                pool.tensor_tensor(qm[u % 2], qT[:, g // 2, i * P:(i + 1) * P].unsqueeze(1).broadcast_to([P, 4, P]),
                                   hmask[:, 4 * (g % 2):4 * (g % 2) + 4].unsqueeze(2).broadcast_to([P, 4, P]),
                                   ALU.mult).then_inc(S["pool_qm"], 1)
            for i in range(NT):
                pool.wait_ge(S["dve_dt"], 3)
                if i >= 1:
                    pool.wait_ge(S["pe_seg"], i)
                pool.tensor_tensor(stp, dAj[:, i, :, :].unsqueeze(3).broadcast_to([P, NC, HG, Q]),
                                   step[:].unsqueeze(1).unsqueeze(1).broadcast_to([P, NC, HG, Q]),
                                   ALU.mult).then_inc(S["pool_stp"], 1)
                if i >= 1:
                    pool.wait_ge(S["pe_e"], i)
                pool.tensor_copy(dAe.rearrange("p (h j q) -> p h j q", h=HG, j=4),
                                 dA[:, i, :].rearrange("p (j h) -> p h j", j=4).unsqueeze(3).broadcast_to([P, HG, 4, SP_]))\
                    .then_inc(S["pool_dae"], 1)

        @block.scalar
        def _(act):
            done = chained(act, "act_self")
            sc = nc.scalar
            act.wait_ge(ld["small"], 48)
            done(sc.activation(ew[:], wu[:, :, 0, :], ACT.Exp))
            sc.activation(ew[:], ew[:], ACT.Exp, scale=-1.0).then_inc(S["act_exw"], 1)
            act.wait_ge(S["pe_cond"], 1)
            sc.activation(tf[:], bank(7, B), ACT.Sigmoid).then_inc(S["act_cond"], 1)
            act.wait_ge(S["dve_uk"], 1)
            sc.activation(ek, ek, ACT.Exp).then_inc(S["act_ek"], 1)
            for i in range(8):
                act.wait_ge(S["dve_uk"], i + 2)
                sc.activation(euk[i % 2], euk[i % 2], ACT.Exp).then_inc(S["act_euk"], 1)
            act.wait_ge(S["dve_winv"], 1)
            for w in range(3):
                sc.activation(wraw[:, w, :], wraw[:, w, :], ACT.Tanh, scale=winv[:, w:w + 1]).then_inc(S["act_tanh"], 1)
            act.wait_ge(S["dve_ln"], 1)
            sc.activation(wat[:], wtmp[:], ACT.Ln).then_inc(S["act_atanh"], 1)

            def sigmoid_x(m):
                act.wait_ge(ld["x"], 16)
                if m:
                    act.wait_ge(S["dve_x"], [0, X_ATT, X_FFN, X_SSD][m])
                sc.activation(A[:], xT[:], ACT.Sigmoid).then_inc(S["act_sg"], 1)

            sigmoid_x(0)
            for i in range(4):
                act.wait_ge(S["pe_q"], i + 1)
                sc.activation(qT[:, i // 2, (i % 2) * HALF:(i % 2 + 1) * HALF], bank(i % 2), ACT.Copy,
                              scale=HD ** -0.5).then_inc(S["act_q"], 1)

            def pt_copy(u):
                tt = (u // 4) % 2
                act.wait_ge(S["pe_pt"], u + 1)
                if u >= 2:
                    act.wait_ge(S["pe_z"], u - 1)
                n = 512 * (tt + 1)
                sc.activation(pt[u % 2][:, 0:n], PSB[:, 4 * HALF:4 * HALF + n], ACT.Copy).then_inc(S["act_pt"], 1)
                if u % 4 == 3:
                    i = u // 4
                    if i >= 1:
                        zt_copy(i - 1)

            def zt_copy(i):
                act.wait_ge(S["pe_zt"], i + 1)
                sc.activation(zT[:, :, i * P:(i + 1) * P], PS[:, 7, 0:256].rearrange("p (a n) -> p a n", a=2),
                              ACT.Copy).then_inc(S["act_zt"], 1)

            for u in range(32):
                g, tt = u % 4, (u // 4) % 2
                n = P * (tt + 1)
                act.wait_ge(S["dve_max"], u + 1)
                if u >= 2:
                    act.wait_ge(S["pe_pt"], u - 1)
                if u >= 8 and g == 0:
                    act.wait_ge(S["dve_zn"], u // 4 - 1)
                for j in range(4):
                    sc.activation(pr[u % 2][:, j, 0:n], PS[:, 2 * (u % 2) + j // 2, (j % 2) * 256:(j % 2) * 256 + n],
                                  ACT.Exp, bias=nmx[:, u % 2, j:j + 1],
                                  accum_out=rsum[:, (u // 4) % 2, 4 * g + j:4 * g + j + 1]).then_inc(S["act_exp"], 1)
                if u >= 1:
                    pt_copy(u - 1)
            pt_copy(31)
            zt_copy(7)

            sigmoid_x(1)
            for i in range(NT):
                act.wait_ge(S["dve_atok"], i + 1)
                done(sc.activation(yq[:, i, :], atok[:, i, :], ACT.Square, accum_out=small[:, 0, i:i + 1]), "act_ss")
            act.wait_ge(S["dve_var"], 1)
            sc.activation(small[:, 1, :], small[:, 2, :], ACT.Sqrt).then_inc(S["act_sqrt"], 1)
            for l in range(2):
                for k in range(4):
                    act.wait_ge(S["pe_xqt"], 4 * l + k + 1)
                    sc.activation(xqT[l][:, :, k * 256:(k + 1) * 256],
                                  PS[:, k, 0:256].bitcast(BF).rearrange("p (a n) -> p a n", a=2),
                                  ACT.Copy).then_inc(S["act_xqt"], 1)
            for i in range(NT):
                act.wait_ge(S["pe_h"], i + 1)
                if i >= 2:
                    act.wait_ge(S["dve_h"], i - 1)
                sc.activation(sw[i % 2], PSB[:, (4 * (i % 2)) * HALF:(4 * (i % 2) + 2) * HALF], ACT.Silu,
                              scale=small[:, 6, i:i + 1]).then_inc(S["act_sw"], 1)
                if i >= 1:
                    act.wait_ge(S["dve_h"], i)
                    done(sc.activation(y3[0], hh[:, i - 1, :], ACT.Square, accum_out=small[:, 8, i - 1:i]), "act_ss3")
            act.wait_ge(S["dve_h"], NT)
            done(sc.activation(y3[0], hh[:, NT - 1, :], ACT.Square, accum_out=small[:, 8, NT - 1:NT]), "act_ss3")
            act.wait_ge(S["dve_var"], 2)
            sc.activation(small[:, 9, :], small[:, 10, :], ACT.Sqrt).then_inc(S["act_sqrt"], 1)
            for i in range(NT):
                act.wait_ge(S["pe_hqt"], i + 1)
                if i >= 2:
                    act.wait_ge(S["pe_o"], i - 1)
                sc.activation(hqT[i % 2], PS[:, i % 2, :].bitcast(BF).rearrange("p (k n) -> p k n", k=HT),
                              ACT.Copy).then_inc(S["act_hqt"], 1)
                act.wait_ge(S["pe_o"], i + 1)
                if i >= 2:
                    act.wait_ge(S["pe_ot"], i - 1)
                sc.activation(otok[i % 2], bank(2 + i % 2, D), ACT.Copy, scale=small[:, 14, i:i + 1])\
                    .then_inc(S["act_o"], 1)

            sigmoid_x(2)
            act.wait_ge(ld["ssd"], 160)
            done(sc.activation(anegb[:], alog[:], ACT.Exp))
            done(sc.activation(anegj[:], alogj[:], ACT.Exp), "act_exw")
            for k in range(8):
                act.wait_ge(S["pe_gate"], k + 1)
                sc.activation(sg[:, k // 2, (k % 2) * HALF:(k % 2 + 1) * HALF], bank(k % 2), ACT.Silu)\
                    .then_inc(S["act_gate"], 1)
            for k in range(6):
                act.wait_ge(S["pe_xbc"], k + 1)
                done(sc.activation(xc[:, k, :], PSB[:, (2 + 2 * (k % 2)) * HALF:(4 + 2 * (k % 2)) * HALF], ACT.Identity,
                                   scale=convw[:, k, 3:4], bias=convb[:, k:k + 1]), "act_cv")
                act.wait_ge(S["dve_cv"], k + 1)
                sc.activation(xc[:, k, :], xc[:, k, :], ACT.Silu).then_inc(S["act_xc"], 1)
            act.wait_ge(S["dve_dtx"], 1)
            done(sc.activation(ddt, dt, ACT.Abs))
            done(sc.activation(ddt, ddt, ACT.Exp, scale=-1.0))
            sc.activation(ddt, ddt, ACT.Ln, bias=1.0).then_inc(S["act_sp2"], 1)
            act.wait_ge(S["pe_dec"], 1)
            sc.activation(t1, bank(0), ACT.Exp).then_inc(S["act_dec"], 1)
            sc.activation(cd.rearrange("p c i h -> p (c i h)"), PSB[:, HALF:5 * HALF], ACT.Exp).then_inc(S["act_cd"], 1)
            for i in range(NT):
                act.wait_ge(S["pe_seg"], i + 1)
                if i >= 1:
                    act.wait_ge(S["pe_yd"], i)
                sc.activation(lm.rearrange("p c h t -> p (c h t)"), PSB[:, 0:4 * HALF], ACT.Exp)\
                    .then_inc(S["act_seg"], 1)
                act.wait_ge(S["pe_e"], i + 1)
                if i >= 1:
                    act.wait_ge(S["dve_y"], i)
                sc.activation(es, PS[:, 6, :], ACT.Exp).then_inc(S["act_e"], 1)
            for k in range(XT):
                act.wait_ge(S["dve_hg"], k + 1)
                sc.activation(xc[:, k, :], ya[:, k, :], ACT.Square).then_inc(S["act_hg2"], 1)
                sc.activation(sg[:, k, :], ya[:, k, :], ACT.Copy, scale=normw[:, k:k + 1]).then_inc(S["act_hgw"], 1)
            act.wait_ge(S["dve_v2"], 1)
            sc.activation(rs, rs, ACT.Sqrt).then_inc(S["act_sq2"], 1)

            sigmoid_x(3)
            act.wait_ge(S["dve_lg"], 1)
            sc.activation(pe8[:], lg[:], ACT.Exp).then_inc(S["act_pe"], 1)
            act.wait_ge(S["pe_ewt"], 1)
            sc.activation(ewT, PS[0:NE, 0:2, :].rearrange("p b n -> p (b n)"), ACT.Copy).then_inc(S["act_ewt"], 1)
            for k in range(16):
                act.wait_ge(S["pe_ewb"], k + 1)
                sc.activation(ewb[:, k // 2, (k % 2) * HALF:(k % 2 + 1) * HALF], bank(k % 2), ACT.Copy)\
                    .then_inc(S["act_ewb"], 1)
            for k in range(2 * MT):
                act.wait_ge(S["pe_up"], k + 1)
                if k >= 2:
                    act.wait_ge(S["dve_hw"], k - 1)
                sc.activation(hs[k % 2], bank(2 * (k % 2)), ACT.Silu).then_inc(S["act_hs"], 1)

        @block.vector
        def _(dve):
            done = chained(dve, "dve_self")
            v = nc.vector
            dve.wait_ge(ld["f"], 16)
            done(v.tensor_scalar(ek, fT, 30.0, None, ALU.min), "dve_uk")
            dve.wait_ge(ld["small"], 48)

            def shifted(i):
                m, ct = divmod(i, 2)
                done(v.tensor_scalar(euk[i % 2], fT[:, ct, :], wu[:, m, 1, ct:ct + 1], 30.0, ALU.add, ALU.min), "dve_uk")

            shifted(0)
            dve.wait_ge(S["act_ek"], 1)
            done(v.tensor_tensor(ekv, ek, fT, ALU.mult))
            dve.wait_ge(S["act_exw"], 1)
            dve.wait_ge(S["act_cond"], 1)
            done(v.tensor_scalar(hf[:], tf[:], 0.5, 0.5, ALU.mult, ALU.add))
            done(v.tensor_scalar(cb[:], tf[:], 0.2, 0.8, ALU.mult, ALU.add))
            done(v.tensor_tensor(dec[:], ew[:].unsqueeze(3).broadcast_to([P, 4, CT, B]),
                                 hf[:].unsqueeze(1).unsqueeze(1).broadcast_to([P, 4, CT, B]), ALU.mult))
            for i in range(8):
                m, ct = divmod(i, 2)
                for b in range(B):
                    r = slice(b * T, (b + 1) * T)
                    d0 = dec[:, m, ct, b:b + 1].broadcast_to([P, T])
                    for fwd, bwd, src in ((nf, nb, ekv), (df, db, ek)):
                        s = src[:, ct, r]
                        done(v.tensor_tensor_scan(fwd[:, r], d0, s, 0.0, ALU.mult, ALU.add))
                        done(v.tensor_tensor_scan(bwd[:, r][:, ::-1], d0, s[:, ::-1], 0.0, ALU.mult, ALU.add))
                if i + 1 < 8:
                    shifted(i + 1)
                dve.wait_ge(S["act_euk"], i + 1)
                done(v.tensor_tensor(gg, euk[i % 2], ek[:, ct, :], ALU.subtract))
                done(v.tensor_tensor(gf, gg, fT[:, ct, :], ALU.mult))
                done(v.tensor_tensor(nf, nf, nb, ALU.add))
                done(v.tensor_tensor(nf, nf, gf, ALU.add))
                done(v.tensor_tensor(df, df, db, ALU.add))
                done(v.tensor_tensor(df, df, gg, ALU.add))
                done(v.tensor_scalar(df, df, 1e-8, None, ALU.max))
                done(v.reciprocal(df, df))
                for b in range(B):
                    r = slice(b * T, (b + 1) * T)
                    done(v.scalar_tensor_tensor(R[:, m, ct, r], nf[:, r], cb[:, b:b + 1], df[:, r], ALU.mult, ALU.mult))
            dve.wait_ge(ld["ffn"], 64)
            for w in range(3):
                done(v.tensor_reduce(wabs[:, w:w + 1], wraw[:, w, :], X, ALU.add, apply_absolute_value=True), "dve_wabs")
            dve.wait_ge(S["pe_wsum"], 1)
            done(v.tensor_scalar(wsc[:], bank(6, 3), 1.0 / (D * H), None, ALU.mult))
            done(v.tensor_scalar(winv[:], wsc[:], 1e-8, None, ALU.add))
            done(v.reciprocal(winv[:], winv[:]), "dve_winv")
            done(v.tensor_scalar(wtmp[:], wsc[:], -1.0, 1.0, ALU.mult, ALU.add))
            done(v.reciprocal(wtmp[:], wtmp[:]))
            done(v.tensor_scalar(wsc[:], wsc[:], 1.0, None, ALU.add))
            done(v.tensor_tensor(wtmp[:], wtmp[:], wsc[:], ALU.mult), "dve_ln")
            for w in range(3):
                dve.wait_ge(S["act_tanh"], w + 1)
                done(v.tensor_scalar(wter[:, w, :], wraw[:, w, :], MAGIC, MAGIC, ALU.add, ALU.subtract), "dve_tern")

            def gate(m):
                dve.wait_ge(S["act_sg"], m + 1)
                done(v.tensor_tensor(A[:], A[:], R[:, m, :, :], ALU.mult), "dve_A")

            dve.wait_ge(ld["const"], 7 * 16)
            done(v.tensor_copy(identb[:], ident[:]))
            done(v.tensor_copy(negmask[:], negmaskf))
            gate(0)
            for i in range(4):
                dve.wait_ge(S["pe_k"], i + 1)
                done(v.tensor_copy(kT[:, i // 2, (i % 2) * HALF:(i % 2 + 1) * HALF], bank(2 + i % 2)), "dve_k")
            for i in range(NT):
                dve.wait_ge(S["pe_v"], i + 1)
                done(v.tensor_copy(vv[:, i, :], bank(4 + i % 4, D)), "dve_v")

            def normalise(i):
                dve.wait_ge(S["act_exp"], 16 * (i + 1))
                done(v.reciprocal(rinv[:, i % 2, :], rsum[:, i % 2, :]))
                dve.wait_ge(S["pe_z"], 4 * (i + 1))
                if i >= 2:
                    dve.wait_ge(S["pe_zt"], i - 1)
                done(v.tensor_tensor(zn[i % 2].rearrange("p (h d) -> p h d", h=NH),
                                     PS[:, 6, 0:D].rearrange("p (h d) -> p h d", h=NH),
                                     rinv[:, i % 2, :].unsqueeze(2).broadcast_to([P, NH, HD]), ALU.mult), "dve_zn")

            for u in range(32):
                tt = (u // 4) % 2
                dve.wait_ge(S["pe_sc"], u + 1)
                if u >= 2:
                    dve.wait_ge(S["act_exp"], 4 * (u - 1))
                src = PSB[:, 2 * (u % 2) * HALF:(2 * (u % 2) + 2) * HALF].rearrange("p (j s) -> p j s", j=4)
                done(v.tensor_reduce(nmx[:, u % 2, :], src[:, :, 0:P * (tt + 1)], X, ALU.max, negate=True), "dve_max")
                if u % 4 == 2 and u >= 4:
                    normalise(u // 4 - 1)
            normalise(7)

            def add_x(psum, mt, ch, name):
                sl = xT[:, mt, ch * HALF:(ch + 1) * HALF]
                done(v.tensor_tensor(sl, sl, psum, ALU.add), name)

            for k in range(4):
                dve.wait_ge(S["pe_wo"], k + 1)
                add_x(bank(k), k // 2, k % 2, "dve_x")

            gate(1)
            dve.wait_ge(ld["ffn"], 64)
            for i in range(NT):
                dve.wait_ge(S["pe_at"], i + 1)
                done(v.tensor_copy(atok[:, i, :], bank(i % 4, D)), "dve_atok")

            def variance(scratch, ss, n, eps):
                done(v.tensor_scalar(scratch, ss, 1.0 / n, eps, ALU.mult, ALU.add), "dve_var")

            dve.wait_ge(S["act_ss"], NT)
            variance(small[:, 2, :], small[:, 0, :], D, 1e-8)
            dve.wait_ge(S["act_sqrt"], 1)
            done(v.reciprocal(small[:, 3, :], small[:, 1, :]))
            dve.wait_ge(S["act_atanh"], 1)
            done(v.tensor_scalar(wat[:], wat[:], 0.5 / 127.0, None, ALU.mult))
            for l in range(2):
                def b8(s):
                    return s.unsqueeze(2).broadcast_to([P, NT, D])
                gl = gb[:, l * D:(l + 1) * D].unsqueeze(1).broadcast_to([P, NT, D])
                done(v.tensor_tensor(yy, atok, b8(small[:, 3, :]), ALU.mult))
                done(v.tensor_tensor(yy, yy, gl, ALU.mult))
                done(v.tensor_reduce(small[:, 4, :], yy, X, ALU.max, apply_absolute_value=True))
                done(v.tensor_scalar(small[:, 4, :], small[:, 4, :], 1e-4, None, ALU.max))
                done(v.reciprocal(small[:, 5, :], small[:, 4, :]))
                done(v.tensor_scalar(small[:, 5, :], small[:, 5, :], 127.0, None, ALU.mult))
                done(v.tensor_scalar(small[:, 6 + l, :], small[:, 4, :], wat[:, l:l + 1], None, ALU.mult))
                done(v.tensor_tensor(yq, yy, b8(small[:, 5, :]), ALU.mult))
                if l:
                    dve.wait_ge(S["pe_xqt"], 4)
                done(v.tensor_scalar(yq, yq, MAGIC, MAGIC, ALU.add, ALU.subtract))
                done(v.tensor_scalar(xqb, yq, -128.0, 127.0, ALU.max, ALU.min), "dve_xq")
            for i in range(NT):
                dve.wait_ge(S["act_sw"], i + 1)
                done(v.scalar_tensor_tensor(hh[:, i, :], PSB[:, (4 * (i % 2) + 2) * HALF:(4 * (i % 2) + 4) * HALF],
                                            small[:, 7, i:i + 1], sw[i % 2], ALU.mult, ALU.mult), "dve_h")
            dve.wait_ge(S["act_ss3"], NT)
            variance(small[:, 10, :], small[:, 8, :], H, 1e-8)
            dve.wait_ge(S["act_sqrt"], 2)
            done(v.reciprocal(small[:, 11, :], small[:, 9, :]))

            def add_tok(i):
                dve.wait_ge(S["pe_ot"], i + 1)
                sl = xT[:, :, i * P:(i + 1) * P]
                done(v.tensor_tensor(sl, sl, PS[:, 4 + i % 2, 0:256].rearrange("p (a n) -> p a n", a=2), ALU.add), "dve_x")

            for i in range(NT):
                y = y3[i % 2]
                done(v.scalar_tensor_tensor(y, hh[:, i, :], small[:, 11, i:i + 1], gb[:, 2 * D:2 * D + H],
                                            ALU.mult, ALU.mult))
                done(v.tensor_reduce(small[:, 12, i:i + 1], y, X, ALU.max, apply_absolute_value=True))
                done(v.tensor_scalar(small[:, 12, i:i + 1], small[:, 12, i:i + 1], 1e-4, None, ALU.max))
                done(v.reciprocal(small[:, 13, i:i + 1], small[:, 12, i:i + 1]))
                done(v.tensor_scalar(small[:, 13, i:i + 1], small[:, 13, i:i + 1], 127.0, None, ALU.mult))
                done(v.tensor_scalar(small[:, 14, i:i + 1], small[:, 12, i:i + 1], wat[:, 2:3], None, ALU.mult))
                done(v.tensor_scalar(y, y, small[:, 13, i:i + 1], MAGIC, ALU.mult, ALU.add))
                done(v.tensor_scalar(y, y, MAGIC, 127.0, ALU.subtract, ALU.min))
                if i >= 2:
                    dve.wait_ge(S["pe_hqt"], i - 1)
                done(v.tensor_scalar(hq[i % 2], y, -128.0, None, ALU.max), "dve_hq")
                if i >= 1:
                    add_tok(i - 1)
            add_tok(NT - 1)

            gate(2)
            dve.wait_ge(ld["ssd"], 160)
            dve.wait_ge(S["act_exw"], 2)
            done(v.tensor_scalar(anegb[:], anegb[:], -1.0, None, ALU.mult))
            done(v.tensor_scalar(anegj[:], anegj[:], -1.0, None, ALU.mult))
            done(v.memset(xbd.rearrange("p c h j q -> p (c h j q)"), 0.0))
            for k in range(6):
                dve.wait_ge(S["act_cv"], k + 1)
                o = xc[:, k, :].rearrange("p (b t) -> p b t", b=B)
                s = PSB[:, (2 + 2 * (k % 2)) * HALF:(4 + 2 * (k % 2)) * HALF].rearrange("p (b t) -> p b t", b=B)
                for back in (1, 2, 3):
                    done(v.scalar_tensor_tensor(o[:, :, back:], s[:, :, 0:T - back], convw[:, k, 3 - back:4 - back],
                                                o[:, :, back:], ALU.mult, ALU.add), "dve_cv" if back == 3 else "dve_self")
            dve.wait_ge(S["pe_dt"], 1)
            done(v.tensor_tensor(dt, bank(6).rearrange("p (i h) -> p i h", i=NT),
                                 dtb[:].unsqueeze(1).broadcast_to([P, NT, SH]), ALU.add), "dve_dtx")
            dve.wait_ge(S["act_sp2"], 1)
            done(v.scalar_tensor_tensor(dt, dt, 0.0, ddt, ALU.max, ALU.add))
            done(v.tensor_tensor(dA, dt, anegb[:].unsqueeze(1).broadcast_to([P, NT, SH]), ALU.mult), "dve_dt")
            for j in range(4):
                for c in range(NC):
                    done(v.tensor_copy(dtj[Q * j:Q * j + Q, :, c, :], dt[Q * c:Q * c + Q, :, HG * j:HG * (j + 1)]),
                         "dve_dt" if (j, c) == (3, 3) else "dve_self")
            done(v.tensor_tensor(dAj.rearrange("p i c h -> p (i c) h"), dtj.rearrange("p i c h -> p (i c) h"),
                                 anegj[:].unsqueeze(1).broadcast_to([P, NT * NC, HG]), ALU.mult), "dve_dt")
            dve.wait_ge(S["act_dec"], 1)
            done(v.tensor_tensor(ddt, dt, t1.rearrange("p (i h) -> p i h", i=NT), ALU.mult), "dve_ddt")
            dve.wait_ge(S["act_cd"], 1)

            def nat(w):
                return w.rearrange("p (j h) -> p h j", j=4).unsqueeze(3).broadcast_to([P, HG, 4, SP_])

            def hjp(w):
                return w.rearrange("p (h j q) -> p h j q", h=HG, j=4)

            chunk = 0
            for i in range(NT):
                dve.wait_ge(S["pe_tok"], i + 1)
                if i >= 1:
                    dve.wait_ge(S["pe_yd"], i)
                xt = bank(4)
                done(v.tensor_copy(btok, bank(5, P)))
                done(v.tensor_tensor(hjp(xdd), hjp(xt), nat(ddt[:, i, :]), ALU.mult), "dve_tok")
                for j in range(4):
                    for c in range(NC):
                        done(v.tensor_tensor(xbd[Q * j:Q * j + Q, c, :, j, :],
                                             hjp(xt)[Q * c:Q * c + Q, :, j, :],
                                             dtj[Q * j:Q * j + Q, i, c, :].unsqueeze(2).broadcast_to([Q, HG, SP_]),
                                             ALU.mult), "dve_xbd" if (j, c) == (3, 3) else "dve_self")
                done(v.tensor_tensor(gm, PS[:, 5, 128:256].rearrange("p (c t) -> p c t", c=NC),
                                     step[:].unsqueeze(1).broadcast_to([P, NC, Q]), ALU.mult), "dve_gm")
                dve.wait_ge(S["act_seg"], i + 1)
                done(v.tensor_tensor(lm, lm, gm.unsqueeze(2).broadcast_to([P, NC, HG, Q]), ALU.mult), "dve_m")
                if i % 2 == 0:
                    if i:
                        dve.wait_ge(S["pe_yo"], 4 * i)
                    done(v.memset(st[0], 0.0), "dve_s")
                for c in range(NC):
                    if i % 2 == 1 and c == NC - 1:
                        break
                    dve.wait_ge(S["pe_sl"], 7 * (i // 2) + 4 * (i % 2) + c + 1)
                    n = (c + 1) % 2
                    done(v.tensor_tensor(hjp(st[n]), hjp(st[1 - n]), nat(cd[:, c, i, :]), ALU.mult))
                    done(v.tensor_tensor(st[n], st[n], PS[:, 7, :], ALU.add), "dve_s")
                dve.wait_ge(S["pe_yo"], 4 * (i + 1))
                dve.wait_ge(S["act_e"], i + 1)
                done(v.tensor_tensor(yo, es, PS[:, 6, :], ALU.mult))
                dve.wait_ge(S["pe_yd"], i + 1)
                done(v.tensor_tensor(ya[:, :, i * P:(i + 1) * P], yo.rearrange("p (a n) -> p a n", a=XT),
                                     PS[:, 4, :].rearrange("p (a n) -> p a n", a=XT), ALU.add), "dve_y")
            for k in range(XT):
                done(v.scalar_tensor_tensor(ya[:, k, :], xc[:, k, :], dskip[:, k:k + 1], ya[:, k, :], ALU.mult, ALU.add))
                done(v.tensor_tensor(ya[:, k, :], ya[:, k, :], sg[:, k, :], ALU.mult), "dve_hg")
            dve.wait_ge(S["pe_var"], 2)
            done(v.tensor_scalar(rs, PSB[:, 0:2 * HALF], 1.0 / DIN, 1e-5, ALU.mult, ALU.add), "dve_v2")
            dve.wait_ge(S["act_sq2"], 1)
            done(v.reciprocal(rs, rs), "dve_rs")
            for k in range(4):
                dve.wait_ge(S["pe_op"], k + 1)
                done(v.tensor_tensor(t1, bank(2 + k), rs[:, (k % 2) * HALF:(k % 2 + 1) * HALF], ALU.mult))
                add_x(t1, k // 2, k % 2, "dve_x")

            gate(3)
            dve.wait_ge(S["pe_lg"], 1)
            lp = bank(0, NT * NE).rearrange("p (i e) -> p i e", i=NT)
            done(v.tensor_reduce(mx8[:], lp, X, ALU.max))
            b8e = [P, NT, NE]
            done(v.tensor_tensor(lg[:], lp, mx8[:].unsqueeze(2).broadcast_to(b8e), ALU.subtract), "dve_lg")
            dve.wait_ge(S["act_pe"], 1)
            for i in range(NT):
                done(v.max(top[:, i, :], pe8[:, i, :]))
                done(v.max_index(tix[:, i, :], top[:, i, :], pe8[:, i, :]))
            done(v.tensor_copy(tixf[:], tix[:]))
            done(v.tensor_tensor(mx8[:], top[:, :, 0], top[:, :, 1], ALU.add))
            done(v.reciprocal(mx8[:], mx8[:]))
            done(v.tensor_tensor(lg[:], top[:], mx8[:].unsqueeze(2).broadcast_to(b8e), ALU.mult))
            io = iota[:].unsqueeze(1).broadcast_to(b8e)
            for s in range(2):
                dst = ewt if s == 0 else ewm
                done(v.tensor_tensor(dst[:], io, tixf[:, :, s:s + 1].broadcast_to(b8e), ALU.is_equal))
                done(v.tensor_tensor(dst[:], dst[:], lg[:, :, s:s + 1].broadcast_to(b8e), ALU.mult))
            done(v.tensor_tensor(ewt[:], ewt[:], ewm[:], ALU.add), "dve_ew")
            for k in range(2 * MT):
                i, ch = divmod(k, 2)
                dve.wait_ge(S["act_hs"], k + 1)
                done(v.tensor_tensor(hs[k % 2], hs[k % 2], bank(2 * (k % 2) + 1), ALU.mult))
                if k >= 4:
                    dve.wait_ge(S["pe_dn"], (k - 4) // 2 + 1)
                if k == 0:
                    dve.wait_ge(S["act_ewb"], 16)
                first, last = i * P // FF, (i * P + P - 1) // FF
                cols = slice(ch * HALF, (ch + 1) * HALF)
                cut = (last * FF - i * P) if first != last else P
                if first != last:
                    done(v.tensor_tensor(hw[k % 4][cut:P, :], hs[k % 2][cut:P, :], ewb[cut:P, last, cols], ALU.mult))
                done(v.tensor_tensor(hw[k % 4][0:cut, :], hs[k % 2][0:cut, :], ewb[0:cut, first, cols], ALU.mult), "dve_hw")
            for k in range(4):
                dve.wait_ge(S["pe_dn"], MT)
                add_x(bank(4 + k), k // 2, k % 2, "dve_out")

        @block.tensor
        def _(pe):
            mm = nc.tensor.matmul

            def acc(dst, pairs, name=None):
                for n, (l, r) in enumerate(pairs):
                    last = mm(dst, l, r, start=(n == 0), stop=(n == len(pairs) - 1))
                if name:
                    last.then_inc(S[name], 1)
                return last

            pe.wait_ge(ld["small"], 48)
            acc(bank(7, B), [(ones[0:64, :], condT[:, :])], "pe_cond")
            pe.wait_ge(S["dve_wabs"], 3)
            acc(bank(6, 3), [(ones[:], wabs[:])], "pe_wsum")

            pe.wait_ge(ld["attn"], 32)
            pe.wait_ge(ld["const"], 7 * 16)
            pe.wait_ge(S["dve_A"], 1)
            for mt in range(CT):
                for qk in range(2):
                    for ch in range(NCH):
                        if mt:
                            pe.wait_ge(S["act_q" if qk == 0 else "dve_k"], ch + 1)
                        acc(bank(2 * qk + ch), [(wqkvo[:, qk, kt, mt * P:(mt + 1) * P], A[:, kt, ch * HALF:(ch + 1) * HALF])
                                                for kt in range(CT)], "pe_q" if qk == 0 else "pe_k")
            pe.wait_ge(S["act_cond"], 1)
            pe.wait_ge(S["dve_winv"], 1)
            for i in range(NT):
                if i >= 4:
                    pe.wait_ge(S["dve_v"], i - 3)
                acc(bank(4 + i % 4, D), [(A[:, kt, i * P:(i + 1) * P], wqkvo[:, 2, kt, :]) for kt in range(CT)], "pe_v")

            def scores(u):
                i, g = divmod(u, 4)
                b, tt = divmod(i, 2)
                n = P * (tt + 1)
                if u >= 2:
                    pe.wait_ge(S["act_exp"], 4 * (u - 1))
                pe.wait_ge(S["pool_qm"], u + 1)
                for j in range(4):
                    o = PS[:, 2 * (u % 2) + j // 2, (j % 2) * 256:(j % 2) * 256 + n]
                    mm(o, qm[u % 2][:, j, :], kT[:, g // 2, b * T:b * T + n], start=True, stop=False)
                    last = mm(o[:, tt * P:n], identb[:], negmask[:], start=False, stop=True)
                last.then_inc(S["pe_sc"], 1)

            def turn(u):
                tt = (u // 4) % 2
                pe.wait_ge(S["act_exp"], 4 * (u + 1))
                if u >= 1:
                    pe.wait_ge(S["act_pt"], u)
                for j in range(4):
                    for k in range(tt + 1):
                        c = (j * (tt + 1) + k) * P
                        last = nc.tensor.transpose(PSB[:, 4 * HALF + c:4 * HALF + c + P],
                                                   pr[u % 2][:, j, k * P:(k + 1) * P], ident[:])
                last.then_inc(S["pe_pt"], 1)

            def values(u):
                i, g = divmod(u, 4)
                b, tt = divmod(i, 2)
                pe.wait_ge(S["act_pt"], u + 1)
                if g == 0 and i >= 1:
                    pe.wait_ge(S["dve_zn"], i)
                for j in range(4):
                    h = 4 * g + j
                    last = acc(PS[:, 6, h * HD:(h + 1) * HD],
                               [(pt[u % 2][:, (j * (tt + 1) + k) * P:(j * (tt + 1) + k + 1) * P],
                                 vv[:, 2 * b + k, h * HD:(h + 1) * HD]) for k in range(tt + 1)])
                last.then_inc(S["pe_z"], 1)

            def turn_z(i):
                pe.wait_ge(S["dve_zn"], i + 1)
                if i >= 1:
                    pe.wait_ge(S["act_zt"], i)
                for ct in range(CT):
                    last = nc.tensor.transpose(PS[:, 7, ct * P:(ct + 1) * P], zn[i % 2][:, ct * P:(ct + 1) * P], ident[:])
                last.then_inc(S["pe_zt"], 1)

            pe.wait_ge(S["act_q"], 4)
            pe.wait_ge(S["dve_k"], 4)
            pe.wait_ge(S["dve_v"], 8)
            for u in range(34):
                if u < 32:
                    scores(u)
                if 1 <= u < 33:
                    turn(u - 1)
                if u >= 2:
                    values(u - 2)
                if u >= 6 and u % 4 == 2:
                    turn_z(u // 4 - 1)
            turn_z(7)
            pe.wait_ge(S["act_zt"], 8)
            for mt in range(CT):
                for ch in range(NCH):
                    acc(bank(2 * mt + ch), [(wqkvo[:, 3, kt, mt * P:(mt + 1) * P], zT[:, kt, ch * HALF:(ch + 1) * HALF])
                                            for kt in range(CT)], "pe_wo")

            pe.wait_ge(S["dve_A"], 2)
            for i in range(NT):
                if i >= 4:
                    pe.wait_ge(S["dve_atok"], i - 3)
                for ct in range(CT):
                    last = nc.tensor.transpose(PS[:, i % 4, ct * P:(ct + 1) * P], A[:, ct, i * P:(i + 1) * P], ident[:])
                last.then_inc(S["pe_at"], 1)
            pe.wait_ge(S["dve_atok"], NT)
            for l in range(2):
                pe.wait_ge(S["dve_xq"], l + 1)
                for k in range(4):
                    if l:
                        pe.wait_ge(S["act_xqt"], k + 1)
                    o = PS[:, k, 0:256].bitcast(BF)
                    for ct in range(CT):
                        for h in range(2):
                            last = nc.tensor.transpose(o[:, ct * 256 + h * P:ct * 256 + (h + 1) * P],
                                                       xqb[:, 2 * k + h, ct * P:(ct + 1) * P], identb[:])
                    last.then_inc(S["pe_xqt"], 1)
            pe.wait_ge(S["act_xqt"], 8)
            pe.wait_ge(S["dve_tern"], 3)
            for i in range(NT):
                if i >= 2:
                    pe.wait_ge(S["dve_h"], i - 1)
                for l in range(2):
                    for hf_ in range(2):
                        last = acc(bank(4 * (i % 2) + 2 * l + hf_),
                                   [(xqT[l][:, ct, i * P:(i + 1) * P],
                                     wter[:, l, ct * H + hf_ * HALF:ct * H + (hf_ + 1) * HALF]) for ct in range(CT)])
                last.then_inc(S["pe_h"], 1)
            pe.wait_ge(S["dve_h"], NT)
            for i in range(NT + 1):
                if i < NT:
                    pe.wait_ge(S["dve_hq"], i + 1)
                    if i >= 2:
                        pe.wait_ge(S["act_hqt"], i - 1)
                    o = PS[:, i % 2, :].bitcast(BF)
                    for k in range(HT):
                        last = nc.tensor.transpose(o[:, k * P:(k + 1) * P], hq[i % 2][:, k * P:(k + 1) * P], identb[:])
                    last.then_inc(S["pe_hqt"], 1)
                    pe.wait_ge(S["act_hqt"], i + 1)
                    if i >= 2:
                        pe.wait_ge(S["act_o"], i - 1)
                    acc(bank(2 + i % 2, D), [(hqT[i % 2][:, k, :], wter[:, 2, k * D:(k + 1) * D]) for k in range(HT)], "pe_o")
                if i >= 1:
                    k = i - 1
                    pe.wait_ge(S["act_o"], k + 1)
                    if k >= 2:
                        pe.wait_ge(S["dve_x"], X_ATT + k - 1)
                    for ct in range(CT):
                        last = nc.tensor.transpose(PS[:, 4 + k % 2, ct * P:(ct + 1) * P],
                                                   otok[k % 2][:, ct * P:(ct + 1) * P], ident[:])
                    last.then_inc(S["pe_ot"], 1)

            pe.wait_ge(ld["ssd"], 160)
            pe.wait_ge(S["dve_A"], 3)
            for k in range(8):
                mt, ch = divmod(k, 2)
                if k >= 2:
                    pe.wait_ge(S["act_gate"], k - 1)
                acc(bank(ch), [(inproj[:, kt, mt * P:(mt + 1) * P], A[:, kt, ch * HALF:(ch + 1) * HALF])
                               for kt in range(CT)], "pe_gate")
            for k in range(6):
                if k >= 2:
                    pe.wait_ge(S["dve_cv"], k - 1)
                c0 = DIN + k * P
                for ch in range(NCH):
                    last = acc(bank(2 + 2 * (k % 2) + ch), [(inproj[:, kt, c0:c0 + P], A[:, kt, ch * HALF:(ch + 1) * HALF])
                                                            for kt in range(CT)])
                last.then_inc(S["pe_xbc"], 1)
            for i in range(NT):
                last = acc(PS[:, 6, i * SH:(i + 1) * SH], [(A[:, kt, i * P:(i + 1) * P], inproj[:, kt, PROJ - SH:PROJ])
                                                           for kt in range(CT)])
            last.then_inc(S["pe_dt"], 1)
            pe.wait_ge(S["dve_dt"], 1)
            pe.wait_ge(S["act_gate"], 8)
            pe.wait_ge(S["dve_cv"], 6)
            dAf = dA.rearrange("p i h -> p (i h)")
            acc(bank(0), [(ugt[:], dAf)])
            for c in range(NC):
                last = acc(bank(1 + c), [(cones[:, c, :], dAf)])
            last.then_inc(S["pe_dec"], 1)
            pe.wait_ge(S["act_dec"], 1)
            pe.wait_ge(S["act_cd"], 1)
            pe.wait_ge(S["act_xc"], 6)
            for i in range(NT):
                tok = slice(i * P, (i + 1) * P)
                if i:
                    pe.wait_ge(S["dve_y"], i)
                    pe.wait_ge(S["dve_gm"], i)
                for k in range(XT):
                    nc.tensor.transpose(PS[:, 4, k * P:(k + 1) * P], xc[:, k, tok], ident[:])
                nc.tensor.transpose(PS[:, 5, 0:P], xc[:, 4, tok], ident[:])
                for c in range(NC):
                    cs = slice(i * P + c * Q, i * P + (c + 1) * Q)
                    for j in range(4):
                        last = acc(PS[Q * j:Q * j + Q, 5, 128 + c * Q:128 + (c + 1) * Q], [(xc[:, 4, cs], xc[:, 5, cs])])
                last.then_inc(S["pe_tok"], 1)
                pe.wait_ge(S["pool_stp"], i + 1)
                if i:
                    pe.wait_ge(S["act_seg"], i)
                for c in range(NC):
                    last = acc(bank(c), [(ugt[:], stp[:, c, :, :].rearrange("p h t -> p (h t)"))])
                last.then_inc(S["pe_seg"], 1)
                pe.wait_ge(S["pool_dae"], i + 1)
                for k in range(XT):
                    last = acc(PS[:, 6, k * P:(k + 1) * P],
                               [(dAe[:, k * P:(k + 1) * P], tri[:])])
                last.then_inc(S["pe_e"], 1)
                pe.wait_ge(S["dve_tok"], i + 1)
                pe.wait_ge(S["act_e"], i + 1)
                for c in range(NC):
                    nstate = 8 * (i // 2) + 4 * (i % 2) + c + 1
                    pe.wait_ge(S["dve_s"], nstate)
                    cs = slice(i * P + c * Q, i * P + (c + 1) * Q)
                    if not (i % 2 == 1 and c == NC - 1):
                        r = slice(Q * c, Q * c + Q)
                        acc(bank(7), [(btok[r, :], xdd[r, :])], "pe_sl")
                    for k in range(XT):
                        last = acc(PS[:, 6, k * P + c * Q:k * P + (c + 1) * Q],
                                   [(st[c % 2][:, k * P:(k + 1) * P], xc[:, 5, cs])])
                    last.then_inc(S["pe_yo"], 1)
                pe.wait_ge(S["dve_xbd"], i + 1)
                pe.wait_ge(S["dve_m"], i + 1)
                for c in range(NC):
                    for h in range(HG):
                        last = acc(PS[Q * (h % 4):Q * (h % 4) + Q, 4, (h // 4) * P + c * Q:(h // 4) * P + (c + 1) * Q],
                                   [(xbd[:, c, h, :, :].rearrange("p j q -> p (j q)"), lm[:, c, h, :])])
                last.then_inc(S["pe_yd"], 1)
            for ch in range(NCH):
                pe.wait_ge(S["act_hg2"], 4)
                acc(bank(ch), [(ones[:], xc[:, k, ch * HALF:(ch + 1) * HALF]) for k in range(XT)], "pe_var")
            pe.wait_ge(S["act_hgw"], 4)
            for k in range(4):
                mt, ch = divmod(k, 2)
                acc(bank(2 + k), [(outproj[:, kt, mt * P:(mt + 1) * P], sg[:, kt, ch * HALF:(ch + 1) * HALF])
                                  for kt in range(XT)], "pe_op")

            pe.wait_ge(S["dve_A"], 4)
            for i in range(NT):
                last = acc(PS[:, 0, i * NE:(i + 1) * NE], [(A[:, kt, i * P:(i + 1) * P], wgate[:, kt, :]) for kt in range(CT)])
            last.then_inc(S["pe_lg"], 1)
            pe.wait_ge(S["dve_ew"], 1)
            for i in range(NT):
                last = nc.tensor.transpose(PS[0:NE, i // 4, (i % 4) * P:(i % 4 + 1) * P], ewt[:, i, :], ident[:])
            last.then_inc(S["pe_ewt"], 1)
            pe.wait_ge(S["act_ewt"], 1)
            pe.wait_ge(ld["sele"], 16)
            for k in range(16):
                e, ch = divmod(k, 2)
                if k >= 2:
                    pe.wait_ge(S["act_ewb"], k - 1)
                acc(bank(k % 2), [(sele[:, e, :], ewT[:, ch * HALF:(ch + 1) * HALF])], "pe_ewb")
            pe.wait_ge(S["act_ewb"], 16)

            def down(i):
                pe.wait_ge(S["dve_hw"], 2 * i + 2)
                for k in range(4):
                    mt, ch = divmod(k, 2)
                    last = mm(bank(4 + k), ring[:, i % RING, 512 + mt * P:512 + (mt + 1) * P], hw[(2 * i + ch) % 4],
                              start=(i == 0), stop=(i == MT - 1))
                last.then_inc(S["pe_dn"], 1)

            for i in range(MT):
                pe.wait_ge(ld_ring[i % RING], 16 * (i // RING + 1))
                for ch in range(NCH):
                    k = 2 * i + ch
                    if k >= 2:
                        pe.wait_ge(S["dve_hw"], k - 1)
                    for w in range(2):
                        last = acc(bank(2 * (k % 2) + w),
                                   [(ring[:, i % RING, w * 256 + kt * P:w * 256 + (kt + 1) * P],
                                     A[:, kt, ch * HALF:(ch + 1) * HALF]) for kt in range(CT)])
                    last.then_inc(S["pe_up"], 1)
                if i >= 1:
                    down(i - 1)
            down(MT - 1)


X_ATT = 4
X_FFN = X_ATT + NT
X_SSD = X_FFN + 4


def arrange(x):
    import numpy as np
    f4 = np.float32

    def kt(w):
        return np.ascontiguousarray(w.reshape(-1, P, w.shape[-1]).transpose(1, 0, 2))

    def pv(v):
        return np.ascontiguousarray(v.reshape(-1, P).T)

    def rows(v):
        return np.ascontiguousarray(np.broadcast_to(v, (P,) + v.shape))

    o = {}
    o["xT"] = kt(x["x"].reshape(N, D).T)
    o["fT"] = kt(x["fside_BxSxS_0"].reshape(N, D).T)
    o["condT"] = np.ascontiguousarray(x["cond_512"].T)
    mods = ("L0_cond", "L0_cond2", "L1_cond", "L1_cond2")
    o["wu"] = np.ascontiguousarray(np.stack([np.stack([pv(x[m + "_w"]), pv(x[m + "_u"])], 1) for m in mods], 1))
    att = [kt(x["L0_attn_" + n].T) for n in ("Wq", "Wk", "Wv", "Wo")]
    o["wqkvo"] = np.stack(att, 1)
    o["w1T"] = kt(x["L0_ffn_w1"].T).reshape(P, -1)
    o["w2T"] = kt(x["L0_ffn_w2"].T).reshape(P, -1)
    o["w3T"] = kt(x["L0_ffn_w3"].T).reshape(P, -1)
    o["gb"] = rows(np.concatenate([x["L0_ffn_g1"], x["L0_ffn_g2"], x["L0_ffn_g3"]]))
    w = x["L1_attn_in_proj_w"]
    jh = np.arange(SH).reshape(HG, 4).T.reshape(-1)
    o["inproj"] = kt(np.concatenate([w[:PROJ - SH], w[PROJ - SH:][jh]], 0).T)
    o["outproj"] = kt(x["L1_attn_out_proj_w"].T)
    o["convw"] = kt(x["L1_attn_conv_w"])
    o["convb"] = pv(x["L1_attn_conv_b"])
    o["dtb"] = rows(x["L1_attn_dt_bias"][jh])
    o["alog"] = rows(x["L1_attn_A_log"][jh])
    o["alogj"] = np.repeat(x["L1_attn_A_log"][jh].reshape(4, HG), Q, 0)
    o["dskip"] = pv(np.repeat(x["L1_attn_D"], SP_))
    o["normw"] = pv(x["L1_attn_norm_w"])
    o["wgate"] = kt(x["L1_ffn_w_gate"].T)

    def up(w):
        return w.reshape(MT, P, CT, P).transpose(0, 3, 2, 1).reshape(MT, P, D)
    dn = x["L1_ffn_w2"].transpose(0, 2, 1).reshape(MT, P, D)
    o["moe"] = np.concatenate([up(x["L1_ffn_w1"]), up(x["L1_ffn_w3"]), dn], 2)
    r = np.arange(P)
    o["ident"] = np.eye(P, dtype=f4)
    o["ones"] = np.ones((P, P), f4)
    o["negmask"] = np.where(r[None, :] > r[:, None], -3.3e38, 0.0).astype(f4)
    same = (r[:, None] // Q) == (r[None, :] // Q)
    o["ugt"] = (same & (r[:, None] > r[None, :])).astype(f4)
    o["tri"] = (same & (r[:, None] <= r[None, :])).astype(f4)
    o["cones"] = np.ascontiguousarray(np.broadcast_to(((r[:, None] // Q) == np.arange(NC)[None, :])[:, :, None], (P, NC, P))).astype(f4)
    o["step"] = ((r[:, None] % Q) <= np.arange(Q)[None, :]).astype(f4)
    o["hmask"] = ((r[:, None] // HD) == np.arange(8)[None, :]).astype(f4)
    o["iota"] = rows(np.arange(NE, dtype=f4))
    o["sele"] = np.ascontiguousarray(np.broadcast_to(np.eye(NE, dtype=f4)[:, :, None], (NE, NE, P)))
    return {k: np.ascontiguousarray(v) for k, v in o.items()}


def program(nc, arrays):
    args = {n: nc.dram_tensor("in_" + n, v.shape, mybir.dt.from_np(v.dtype), kind="ExternalInput").ap()
            for n, v in arrays.items()}
    out = nc.dram_tensor("out_0", (P, CT, N), mybir.dt.float32, kind="ExternalOutput").ap()
    build(nc, args, out)


def kernel(**inputs):
    import numpy as np
    import concourse.bacc as bacc
    from concourse.bass_utils import run_bass_kernel_spmd

    arrays = arrange({k: np.asarray(v) for k, v in inputs.items()})
    nc = bacc.Bacc("TRN2", target_bir_lowering=False, num_devices=1)
    program(nc, arrays)
    r = run_bass_kernel_spmd(nc, [{"in_" + n: v for n, v in arrays.items()}], core_ids=[0])
    got = r.results[0]["out_0"]
    return np.ascontiguousarray(got.transpose(1, 0, 2).reshape(D, N).T).reshape(B, T, D)
```

```python
import concourse.bass as bass
from concourse import mybir
from contextlib import ExitStack
from math import exp

P = 128
B, T, D = 4, 256, 256
N = B * T
CT = D // P
NT = N // P
HALF = 512
NCH = N // HALF
NH, HD = 16, 16
VW = HD + 1
G4 = NH // 4
H = 1024
HT = H // P
DIN, NS, SH, SP_ = 512, 128, 64, 8
XT = DIN // P
Q = 32
NC = P // Q
HG = SH // 4
PROJ = DIN + DIN + 2 * NS + SH
NE, FF = 8, 704
MT = NE * FF // P
RING = 4
WRING = 3
E30 = exp(30.0)
MAGIC = 1.5 * 2.0 ** 23


def build(nc, a, routing, out):
    F = mybir.dt.float32
    BF = mybir.dt.bfloat16
    U32 = mybir.dt.uint32
    FR = mybir.dt.float32r
    ALU = mybir.AluOpType
    ACT = mybir.ActivationFunctionType
    X = mybir.AxisListType.X

    with ExitStack() as ctx:
        def sb(name, shape, dt=F):
            return ctx.enter_context(nc.sbuf_tensor(name, shape, dt))

        def sem(name):
            return ctx.enter_context(nc.semaphore(name))

        ARENA = 30 * 1024
        arena_at = (nc.sbuf_base + 31) // 32 * 32
        arena = sb("arena", [P, ARENA])
        K = 1024

        def at(words, n, *dims):
            v = arena[:, words:words + n]
            return v

        xT = sb("xT", [P, CT, N])
        A = sb("A", [P, CT, N])
        R = sb("R", [P, 4, NCH, CT * HALF])
        ident = sb("ident", [P, P])
        identb = sb("identb", [P, P], BF)
        ones = sb("ones", [P, P])
        negmask = sb("negmask", [P, P], BF)
        negmaskf = arena[:, 28 * K:28 * K + P]
        ugt = sb("ugt", [P, P])
        tri = sb("tri", [P, P])
        cones = sb("cones", [P, NC, P])
        step = sb("step", [P, Q])
        notfirst = sb("notfirst", [P, T])
        hmask = sb("hmask", [P, 8])
        iota = sb("iota", [P, NE])
        condT = sb("condT", [64, B])
        wu = sb("wu", [P, 4, 2, CT])
        inproj = sb("inproj", [P, CT, PROJ])
        outproj = sb("outproj", [P, XT, D])
        convw = sb("convw", [P, 6, 4])
        convb = sb("convb", [P, 6])
        dtb = sb("dtb", [P, SH])
        alog = sb("alog", [P, SH])
        alogj = sb("alogj", [P, HG])
        dskip = sb("dskip", [P, XT])
        normw = sb("normw", [P, XT])
        wgate = sb("wgate", [P, CT, NE])
        tf = sb("tf", [P, B])
        hf = sb("hf", [P, B])
        cb = sb("cb", [P, B])
        ew = sb("ewx", [P, 4, CT])
        dec = sb("dec", [P, 4, CT, B])
        wabs = sb("wabs", [P, 3])
        wsc = sb("wsc", [P, 3])
        winv = sb("winv", [P, 3])
        wat = sb("wat", [P, 3])
        wtmp = sb("wtmp", [P, 3])
        ss, root, msq, rms1 = (sb(n, [P, NT]) for n in ("ss", "root", "msq", "rms1"))
        peak, oscale, iscale, ipeak = (sb(n, [P, 2, NT]) for n in ("peak", "oscale", "iscale", "ipeak"))
        ss3, root3, msq3, rms3, peak3, oscale3, iscale3 = \
            (sb(n, [P, NT]) for n in ("ss3", "root3", "msq3", "rms3", "peak3", "oscale3", "iscale3"))

        def halves(o):
            return arena[:, o * K:(o + 2) * K].rearrange("p (a n) -> p a n", a=CT)
        fT, fc, ek, ekv = halves(0), halves(2), halves(4), halves(6)
        o = 18 * K + NT * NH * VW
        sums = [[arena[:, w:w + K] for w in range(8 * K, 13 * K, K)],
                [arena[:, w:w + K] for w in (o, o + K, o + 2 * K, o + 3 * K, 27 * K)]]
        dmat = sb("dmat", [P, N + 1])
        wter = arena[:, 27 * K:30 * K].bitcast(BF).rearrange("p (w n) -> p w n", w=3)
        qT, kT, zT = halves(13), halves(15), A
        qm = [w.rearrange("p (j t) -> p j t", j=4) for w in
              (arena[:, 17 * K:17 * K + 512], arena[:, 17 * K + 512:18 * K], cones[:].rearrange("p c k -> p (c k)"))]
        vv = arena[:, 18 * K:18 * K + NT * NH * VW].rearrange("p (i h d) -> p i h d", i=NT, h=NH)
        o = 18 * K + NT * NH * VW
        pr = [arena[:, o + i * K:o + (i + 1) * K].rearrange("p (j s) -> p j s", j=4) for i in range(2)]
        pt = [arena[:, o + (2 + i) * K:o + (3 + i) * K] for i in range(2)]
        wqkvo = arena[:, o + 4 * K:o + 6 * K].rearrange("p (w k n) -> p w k n", w=4, k=CT)
        zn = [arena[:, o + 6 * K + 256 * i:o + 6 * K + 256 * (i + 1)] for i in range(2)]
        nmx = sb("nmx", [P, 2, 4])
        rinv = sb("rinv", [P, 2, NH])
        gb = arena[:, 0:2 * D + H]
        FO = 2 * D + H

        def ffn(k, words=K):
            return arena[:, FO + k:FO + k + words]
        atok = [ffn(c * K).rearrange("p (i n) -> p i n", i=4) for c in range(2)]
        zz = [[ffn((2 + 2 * c + l) * K).rearrange("p (i n) -> p i n", i=4) for l in range(2)] for c in range(2)]
        zs = [[ffn((o + l) * K).rearrange("p (i n) -> p i n", i=4) for l in range(2)] for o in (6, 12)]
        xqb = [[ffn(8 * K + 512 * (2 * c + l), 512).bitcast(BF).rearrange("p (i n) -> p i n", i=4) for l in range(2)]
               for c in range(2)]
        xqT = [ffn((10 + l) * K).bitcast(BF).rearrange("p (a n) -> p a n", a=CT) for l in range(2)]
        z3 = ffn(12 * K, 8 * K).rearrange("p (i n) -> p i n", i=NT)
        hh = [ffn((20 + i) * K) for i in range(2)]
        sw = [ffn(22 * K + 512 * i, 512) for i in range(2)]
        sq3 = ffn(23 * K)
        y3 = [ffn((2 + i) * K) for i in range(2)]
        hqT = [ffn(4 * K + 512 * i, 512).bitcast(BF).rearrange("p (k n) -> p k n", k=HT) for i in range(2)]
        hq = [ffn(24 * K + 512 * i, 512).bitcast(BF) for i in range(2)]
        otok = [ffn(25 * K + 256 * i, 256) for i in range(2)]
        sg = arena[:, 0:4 * K].rearrange("p (a n) -> p a n", a=XT)
        xc = arena[:, 4 * K:10 * K].rearrange("p (a n) -> p a n", a=6)
        ya = arena[:, 10 * K:14 * K].rearrange("p (a n) -> p a n", a=XT)
        cd = arena[:, 14 * K:16 * K].rearrange("p (c i h) -> p c i h", c=NC, i=NT)
        stp = arena[:, 16 * K:18 * K].rearrange("p (c h t) -> p c h t", c=NC, h=HG)
        done_gate = [R[:, m].rearrange("p c n -> p (c n)") for m in range(3)]
        lm = [w.rearrange("p (c h t) -> p c h t", c=NC, h=HG) for w in
              (arena[:, 18 * K:20 * K], arena[:, 20 * K:22 * K], done_gate[0])]
        spent = inproj[:].rearrange("p a n -> p (a n)")
        xbd = [w.rearrange("p (c h j q) -> p c h j q", c=NC, h=HG, j=4) for w in
               (arena[:, 22 * K:24 * K], spent[:, 0:2 * K], done_gate[1])]
        dt = arena[:, 24 * K:24 * K + 512].rearrange("p (i h) -> p i h", i=NT)
        dAe = arena[:, 24 * K:24 * K + 512]
        t1 = arena[:, 24 * K + 512:25 * K]
        yo = [t1, done_gate[2][:, 0:512]]
        rsb = arena[:, 16 * K:16 * K + 512]
        dA = arena[:, 25 * K:25 * K + 512].rearrange("p (i h) -> p i h", i=NT)
        dtj = arena[:, 25 * K + 512:26 * K].rearrange("p (i c h) -> p i c h", i=NT, c=NC)
        dAj = arena[:, 26 * K:26 * K + 512].rearrange("p (i c h) -> p i c h", i=NT, c=NC)
        ddt = arena[:, 26 * K + 512:27 * K].rearrange("p (i h) -> p i h", i=NT)
        gm = arena[:, 27 * K:27 * K + 128].rearrange("p (c t) -> p c t", c=NC)
        btok = [done_gate[2][:, 512 * (1 + i):512 * (2 + i)].rearrange("p (c n) -> p c n", c=NC) for i in range(2)]
        xdd = [arena[:, 27 * K + 512:28 * K], spent[:, 2 * K:2 * K + 512]]
        es = [arena[:, 28 * K + 512 * i:28 * K + 512 * (i + 1)] for i in range(2)]
        st = [arena[:, 29 * K + 512 * i:29 * K + 512 * (i + 1)] for i in range(2)]
        anegb = sb("anegb", [P, SH])
        hms, hroot, hrms = (sb(n, [P, NT]) for n in ("hms", "hroot", "hrms"))
        anegj = sb("anegj", [P, HG])
        def placed(name, words, shape, dt):
            return nc.alloc_sbuf_tensor_at(name, shape, dt, offset=arena_at + 4 * words)

        ewb = arena[:, 0:8 * K].rearrange("p (e n) -> p e n", e=NE)
        Ah = placed("Ah", 8 * K, [P, CT, N], FR)
        Al = placed("Al", 10 * K, [P, CT, N], FR)
        hw = [arena[:, 12 * K + 512 * i:12 * K + 512 * (i + 1)] for i in range(2)]
        hwh = placed("hwh", 13 * K, [P, 4, HALF], FR)
        hwl = placed("hwl", 15 * K, [P, 4, HALF], FR)
        ewT = arena[0:NE, 17 * K:18 * K]
        ring = arena[:, 18 * K:18 * K + RING * 768].rearrange("p (r n) -> p r n", r=RING)
        wh = placed("wh", 23 * K, [P, WRING, 768], FR)
        wl = placed("wl", 23 * K + WRING * 768, [P, WRING, 768], FR)
        hs = [arena[:, 28 * K + 512 * i:28 * K + 512 * (i + 1)] for i in range(4)]
        lg = sb("lg", [P, NT, NE])
        pe8 = sb("pe8", [P, NT, NE])
        top = sb("top", [P, NT, NE])
        tix = sb("tix", [P, NT, NE], U32)
        tixf = sb("tixf", [P, NT, NE])
        ewt = sb("ewt", [P, NT, NE])
        ewm = sb("ewm", [P, NT, NE])
        mx8 = sb("mx8", [P, NT])

        PS = ctx.enter_context(nc.psum_tensor("PS", [P, 8, HALF], F))
        PSB = PS[:, :, :].rearrange("p b n -> p (b n)")

        def bank(i, n=HALF):
            return PS[:, i, 0:n]

        ld = {k: sem("ld_" + k) for k in ("x", "f", "const", "small", "ffn", "attn", "ssd", "gb", "cones")}
        ld_ring = [sem(f"ld_ring{i}") for i in range(RING)]
        ld_ewb = [sem(f"ld_ewb{e}") for e in range(NE)]
        st_ewt = sem("st_ewt")
        st_out = sem("st_out")
        NAMES = """pool_qm dve_self act_self pool_self pe_cond act_cond dve_fmin act_euk dve_fc dve_den act_guess dve_R dve_scan pool_den pool_num dve_g dve_nf act_wabs act_ek pe_wsum dve_winv
            act_tanh dve_tern act_exw act_atanh dve_ln
            act_sg dve_A pe_q pe_k pe_v act_q dve_k dve_v pe_sc dve_max act_exp pe_pt act_pt pe_z dve_zn pe_zt act_zt pe_wo dve_x
            pe_at act_atok pool_z2 act_ss dve_var act_sqrt dve_scale pool_zs dve_xq pe_xqt act_xqt pe_h act_sw dve_h act_ss3 pool_z3 dve_var3 act_sqrt3 dve_scale3 act_y3 dve_hq pe_hqt act_hqt pe_o act_o pe_ot
            pe_gate act_gate pe_xbc act_cv dve_cv act_xc pe_dt dve_dtx act_sp1 act_sp2 dve_dt pe_dec act_dec act_cd dve_ddt
            pool_zero pe_tok dve_xbd dve_tok pool_stp pool_dae pe_seg act_seg dve_gm pool_m pe_e act_e pe_yd pe_yo dve_yo dve_y pe_sl dve_s
            act_skip dve_hg act_hg2 act_opw pe_var dve_v2 act_sq2 dve_rs pe_rsb pe_op
            pe_lg dve_lg act_pe dve_ew pe_ewb act_ewb pe_ewt act_ewt pe_up act_wh pool_wl act_ah dve_al dve_up pool_hl dve_hh act_hs dve_hw pe_dn dve_out""".split()
        S = {n: sem(n) for n in NAMES}

        def chained(eng, own):
            count = {}

            def done(ins, name=own):
                count[name] = count.get(name, 0) + 1
                ins.then_inc(S[name], 1)
                eng.wait_ge(S[name], count[name])
            return done

        block = ctx.enter_context(nc.Block())

        @block.sync
        def _(sp):
            def load(dst, src, group):
                sp.dma_start(dst, src).then_inc(ld[group], 16)

            load(fT, a["fT"], "f")
            load(wu[:], a["wu"], "small")
            load(condT[:], a["condT"], "small")
            load(ones[:], a["ones"], "small")
            load(notfirst[:], a["notfirst"], "small")
            load(xT[:], a["xT"], "x")
            for w, n in enumerate(("w1T", "w2T", "w3T")):
                load(R[:, 1 + w].rearrange("p c n -> p (c n)"), a[n], "ffn")
            for n, m in (("ident", ident), ("negmask", negmaskf), ("ugt", ugt), ("tri", tri),
                         ("step", step), ("iota", iota)):
                load(m[:], a[n], "const")
            load(wqkvo, a["wqkvo"], "attn")
            load(hmask[:], a["hmask"], "attn")
            for n, m in (("inproj", inproj), ("outproj", outproj), ("convw", convw), ("convb", convb), ("dtb", dtb),
                         ("alog", alog), ("alogj", alogj), ("dskip", dskip), ("normw", normw), ("wgate", wgate)):
                load(m[:], a[n], "ssd")
            sp.wait_ge(S["dve_R"], 8)
            sp.wait_ge(S["act_euk"], 16)
            load(gb, a["gb"], "gb")
            sp.wait_ge(S["pe_sc"], 32)
            load(cones[:], a["cones"], "cones")
            sp.wait_ge(S["pe_yd"], NT)

            def expert(i):
                if i >= RING:
                    sp.wait_ge(S["act_wh"], i - RING + 1)
                    sp.wait_ge(S["pool_wl"], i - RING + 1)
                sp.dma_start(ring[:, i % RING, :], a["moe"][i]).then_inc(ld_ring[i % RING], 16)

            for i in range(RING):
                expert(i)
            sp.wait_ge(S["act_ewt"], 1)
            sp.dma_start(routing, ewT).then_inc(st_ewt, 16)
            sp.wait_ge(st_ewt, 16)
            for e in range(1, NE):
                sp.dma_start(ewb[:, e, :], routing[e:e + 1, :].broadcast_to([P, N])).then_inc(ld_ewb[e], 16)
            for i in range(RING, MT):
                expert(i)
            sp.wait_ge(S["dve_out"], 4)
            sp.dma_start(out, xT[:]).then_inc(st_out, 16)
            sp.wait_ge(st_out, 16)

        @block.gpsimd
        def _(pool):
            done = chained(pool, "pool_self")

            def gate_add(i, k):
                c = i % 2
                g, nf, nb, df, db = sums[i == 1]
                if k == 0:
                    pool.wait_ge(S["dve_scan"], 2 * i + 1)
                    done(pool.tensor_tensor(df, df, db, ALU.add))
                if k == 1:
                    pool.wait_ge(S["dve_g"], i + 1)
                    done(pool.tensor_tensor(df, df, g, ALU.add), "pool_den")
                if k == 2:
                    done(pool.tensor_tensor(g, g, fc[:, c, :], ALU.mult))
                if k == 3:
                    pool.wait_ge(S["dve_nf"], i + 1)
                    done(pool.tensor_tensor(nf, nf, g, ALU.add), "pool_num")

            for i in range(2):
                pool.wait_ge(S["dve_fc"], i + 1)
                for k in range(4):
                    gate_add(i, k)
            pool.wait_ge(ld["attn"], 32)
            pool.wait_ge(S["act_q"], 4)

            def masked(u):
                i, g = divmod(u, 4)
                if u >= QRING:
                    pool.wait_ge(S["pe_sc"], u - QRING + 1)
                pool.tensor_tensor(qm[u % QRING], qT[:, g // 2, i * P:(i + 1) * P].unsqueeze(1).broadcast_to([P, 4, P]),
                                   hmask[:, 4 * (g % 2):4 * (g % 2) + 4].unsqueeze(2).broadcast_to([P, 4, P]),
                                   ALU.mult).then_inc(S["pool_qm"], 1)

            masked(0)
            masked(1)
            for u in range(32):
                if u + 2 < 32:
                    masked(u + 2)
                f, k = divmod(u, FRAME)
                if k >= 2:
                    gate_add(f + 2, k - 2)
                elif k == 0 and f:
                    gate_add(f + 1, 3)
            pool.wait_ge(ld["gb"], 16)

            def per_token(w, c, n):
                return w[:, c * 4:(c + 1) * 4].unsqueeze(2).broadcast_to([P, 4, n])

            for c in range(2):
                pool.wait_ge(S["act_atok"], c + 1)
                pool.tensor_tensor(zz[c][1], atok[c], gb[:, D:2 * D].unsqueeze(1).broadcast_to([P, 4, D]), ALU.mult)\
                    .then_inc(S["pool_z2"], 1)
            pool.wait_ge(S["dve_scale"], 1)
            pool.wait_ge(S["pool_z2"], 2)
            for c in range(2):
                pool.tensor_tensor(zs[c][1], zz[c][1], per_token(iscale[:, 1, :], c, D), ALU.mult).then_inc(S["pool_zs"], 1)
            for i in range(NT):
                pool.wait_ge(S["dve_h"], 2 * i + 2)
                pool.tensor_tensor(z3[:, i, :], hh[i % 2], gb[:, 2 * D:2 * D + H], ALU.mult).then_inc(S["pool_z3"], 1)

            def steps(i):
                if i >= 1:
                    pool.wait_ge(S["pe_seg"], 2 * i)
                pool.tensor_tensor(stp, dAj[:, i, :, :].unsqueeze(3).broadcast_to([P, NC, HG, Q]),
                                   step[:].unsqueeze(1).unsqueeze(1).broadcast_to([P, NC, HG, Q]),
                                   ALU.mult).then_inc(S["pool_stp"], 1)
                if i >= 1:
                    pool.wait_ge(S["pe_e"], i)
                pool.tensor_copy(dAe.rearrange("p (h j q) -> p h j q", h=HG, j=4),
                                 dA[:, i, :].rearrange("p (j h) -> p h j", j=4).unsqueeze(3).broadcast_to([P, HG, 4, SP_]))\
                    .then_inc(S["pool_dae"], 1)

            pool.wait_ge(S["dve_A"], 6)
            pool.memset(xbd[0].rearrange("p c h j q -> p (c h j q)"), 0.0).then_inc(S["pool_zero"], 1)
            pool.wait_ge(S["dve_dt"], 2)
            pool.wait_ge(S["dve_ddt"], 1)
            steps(0)
            pool.wait_ge(S["pe_dt"], 1)
            pool.wait_ge(S["pe_gate"], 8)
            pool.wait_ge(S["pe_xbc"], 6)
            pool.memset(xbd[1].rearrange("p c h j q -> p (c h j q)"), 0.0).then_inc(S["pool_zero"], 1)
            pool.memset(xbd[2].rearrange("p c h j q -> p (c h j q)"), 0.0).then_inc(S["pool_zero"], 1)
            steps(1)
            for i in range(NT):
                pool.wait_ge(S["act_seg"], 2 * i + 2)
                pool.wait_ge(S["dve_gm"], i + 1)
                pool.tensor_tensor(lm[i % MRING], lm[i % MRING], gm.unsqueeze(2).broadcast_to([P, NC, HG, Q]), ALU.mult)\
                    .then_inc(S["pool_m"], 1)
                if i + 2 < NT:
                    steps(i + 2)

            def weights_lo(i):
                pool.wait_ge(S["act_wh"], i + 1)
                pool.tensor_tensor(wl[:, i % WRING, :], ring[:, i % RING, :], wh[:, i % WRING, :], ALU.subtract)\
                    .then_inc(S["pool_wl"], 1)

            weights_lo(0)
            weights_lo(1)
            for k in range(2 * MT):
                pool.wait_ge(S["dve_hh"], k + 1)
                pool.tensor_tensor(hwl[:, k % 4, :], hw[k % 2], hwh[:, k % 4, :], ALU.subtract).then_inc(S["pool_hl"], 1)
                if k % 2 and k // 2 + 2 < MT:
                    weights_lo(k // 2 + 2)

        @block.scalar
        def _(act):
            done = chained(act, "act_self")
            sc = nc.scalar
            LN_EXP = "natural_log_exp_and_others"
            sc.preload_act_table(ACT.Sigmoid)
            act.wait_ge(S["pe_cond"], 1)
            sc.activation(tf[:], bank(7, B), ACT.Sigmoid).then_inc(S["act_cond"], 1)
            sc.preload_act_table_set(LN_EXP)
            act.wait_ge(ld["small"], 64)
            done(sc.activation(ew[:], wu[:, :, 0, :], ACT.Exp))
            sc.activation(ew[:], ew[:], ACT.Exp, scale=-1.0).then_inc(S["act_exw"], 1)
            for ct in range(CT):
                act.wait_ge(S["dve_fmin"], ct + 1)
                sc.activation(ek[:, ct, :], ek[:, ct, :], ACT.Exp).then_inc(S["act_ek"], 1)

            def bonus(i):
                m, c = divmod(i, 2)
                if i >= 2:
                    act.wait_ge(S["pool_num"], 1 if i == 2 else i)
                for ct in range(CT):
                    cols = slice(ct * HALF, (ct + 1) * HALF)
                    sc.activation(sums[i == 1][0][:, cols], fT[:, c, cols], ACT.Exp, bias=wu[:, m, 1, ct:ct + 1])\
                        .then_inc(S["act_euk"], 1)

            def reciprocal_guess(i):
                db, df = sums[i == 1][4], sums[i == 1][3]
                act.wait_ge(S["dve_den"], i + 1)
                done(sc.activation(db, df, ACT.Ln))
                sc.activation(db, db, ACT.Exp, scale=-1.0).then_inc(S["act_guess"], 1)

            bonus(0)
            bonus(1)
            act.wait_ge(ld["ffn"], 48)
            for w in range(3):
                done(sc.activation(A[:].rearrange("p a n -> p (a n)"), R[:, 1 + w].rearrange("p c n -> p (c n)"), ACT.Abs,
                                   accum_out=wabs[:, w:w + 1]), "act_wabs")
            reciprocal_guess(0)

            def sigmoid_x(m, c):
                act.wait_ge(ld["x"], 16)
                if m:
                    act.wait_ge(S["dve_x"], [0, 4, X_ATT + 4, X_FFN + 2][m] + c * [0, 4, 4, 2][m])
                sc.activation(A[:, :, c * HALF:(c + 1) * HALF], xT[:, :, c * HALF:(c + 1) * HALF], ACT.Sigmoid)\
                    .then_inc(S["act_sg"], 1)

            sigmoid_x(0, 0)
            sigmoid_x(0, 1)
            act.wait_ge(S["dve_winv"], 1)
            for w in range(3):
                wv = R[:, 1 + w].rearrange("p c n -> p (c n)")
                sc.activation(wv, wv, ACT.Tanh, scale=winv[:, w:w + 1]).then_inc(S["act_tanh"], 1)
            sc.preload_act_table_set(LN_EXP)
            act.wait_ge(S["dve_ln"], 1)
            sc.activation(wat[:], wtmp[:], ACT.Ln).then_inc(S["act_atanh"], 1)
            reciprocal_guess(1)
            for i in range(4):
                act.wait_ge(S["pe_q"], i + 1)
                sc.activation(qT[:, i % 2, (i // 2) * HALF:(i // 2 + 1) * HALF], bank(i % 2), ACT.Copy,
                              scale=HD ** -0.5).then_inc(S["act_q"], 1)

            def pt_copy(u):
                tt = (u // 4) % 2
                act.wait_ge(S["pe_pt"], u + 1)
                if u >= 2:
                    act.wait_ge(S["pe_z"], u - 1)
                n = 512 * (tt + 1)
                sc.activation(pt[u % 2][:, 0:n], PSB[:, 4 * HALF:4 * HALF + n], ACT.Copy).then_inc(S["act_pt"], 1)
                if u % 4 == 2 and u >= 6:
                    zt_copy(u // 4 - 1)

            def zt_copy(i):
                act.wait_ge(S["pe_zt"], i + 1)
                sc.activation(zT[:, :, i * P:(i + 1) * P], PS[:, 7, 0:256].rearrange("p (a n) -> p a n", a=2),
                              ACT.Copy).then_inc(S["act_zt"], 1)

            for u in range(32):
                g, tt = u % 4, (u // 4) % 2
                n = P * (tt + 1)
                act.wait_ge(S["dve_max"], u + 1)
                if u >= 2:
                    act.wait_ge(S["pe_pt"], u - 1)
                for j in range(4):
                    sc.activation(pr[u % 2][:, j, 0:n], PS[:, 2 * (u % 2) + j // 2, (j % 2) * 256:(j % 2) * 256 + n],
                                  ACT.Exp, bias=nmx[:, u % 2, j:j + 1]).then_inc(S["act_exp"], 1)
                if u >= 1:
                    pt_copy(u - 1)
                i, k = divmod(u, FRAME)
                if k == 1 and i < 6:
                    bonus(i + 2)
                if k == 4:
                    reciprocal_guess(i + 2)
            pt_copy(31)
            zt_copy(7)


            def turned(c):
                for l in range(2):
                    act.wait_ge(S["pe_xqt"], 2 * c + l + 1)
                    sc.activation(xqT[l][:, :, c * HALF:(c + 1) * HALF],
                                  PS[:, 6 - 2 * c + l, :].bitcast(BF).rearrange("p (a n) -> p a n", a=CT), ACT.Copy)\
                        .then_inc(S["act_xqt"], 1)

            def hidden(k):
                act.wait_ge(S["pe_h"], k + 1)
                if k >= 2:
                    act.wait_ge(S["dve_h"], k - 1)
                sc.activation(sw[k % 2], bank(2 * (k % 2)), ACT.Silu, scale=oscale[:, 0, k // 2:k // 2 + 1])\
                    .then_inc(S["act_sw"], 1)

            sigmoid_x(1, 0)
            sigmoid_x(1, 1)
            for c in range(2):
                act.wait_ge(S["pe_at"], c + 1)
                n = (6 - 2 * c) * HALF
                done(sc.activation(atok[c].rearrange("p i n -> p (i n)"), PSB[:, n:n + 2 * HALF], ACT.Copy), "act_atok")
                for i in range(4):
                    done(sc.activation(hh[0][:, 0:D], atok[c][:, i, :], ACT.Square, accum_out=ss[:, 4 * c + i:4 * c + i + 1]),
                         "act_ss")
            act.wait_ge(S["dve_var"], 1)
            sc.activation(root[:], msq[:], ACT.Sqrt).then_inc(S["act_sqrt"], 1)
            turned(0)
            turned(1)
            for s in range(2 * NT):
                if s < NT:
                    hidden(2 * s)
                    hidden(2 * s + 1)
                if 1 <= s <= NT:
                    i = s - 1
                    act.wait_ge(S["dve_h"], 2 * i + 2)
                    done(sc.activation(sq3, hh[i % 2], ACT.Square, accum_out=ss3[:, i:i + 1]), "act_ss3")
                if s in (4, 8):
                    c = s // 4 - 1
                    act.wait_ge(S["dve_var3"], c + 1)
                    sc.activation(root3[:, 4 * c:4 * c + 4], msq3[:, 4 * c:4 * c + 4], ACT.Sqrt).then_inc(S["act_sqrt3"], 1)
                if 0 <= s - 7 < NT:
                    i = s - 7
                    act.wait_ge(S["pe_o"], i + 1)
                    if i >= 2:
                        act.wait_ge(S["pe_ot"], i - 1)
                    sc.activation(otok[i % 2], bank(4, D), ACT.Copy, scale=oscale3[:, i:i + 1]).then_inc(S["act_o"], 1)
                if 0 <= s - 6 < NT:
                    i = s - 6
                    act.wait_ge(S["pe_hqt"], i + 1)
                    if i >= 2:
                        act.wait_ge(S["pe_o"], i - 1)
                    sc.activation(hqT[i % 2], PS[:, 6 + i % 2, :].bitcast(BF).rearrange("p (k n) -> p k n", k=HT),
                                  ACT.Copy).then_inc(S["act_hqt"], 1)
                if 0 <= s - 4 < NT:
                    i = s - 4
                    act.wait_ge(S["dve_scale3"], i // 4 + 1)
                    if i >= 2:
                        act.wait_ge(S["dve_hq"], i - 1)
                    sc.activation(y3[i % 2], z3[:, i, :], ACT.Copy, scale=iscale3[:, i:i + 1]).then_inc(S["act_y3"], 1)
                if s == 12:
                    sigmoid_x(2, 0)

            sigmoid_x(2, 1)
            act.wait_ge(ld["ssd"], 160)
            sc.preload_act_table_set(LN_EXP)
            done(sc.activation(anegb[:], alog[:], ACT.Exp))
            done(sc.activation(anegj[:], alogj[:], ACT.Exp), "act_exw")

            for k in range(XT):
                sc.activation(outproj[:, k, :], outproj[:, k, :], ACT.Copy, scale=normw[:, k:k + 1]).then_inc(S["act_opw"], 1)

            act.wait_ge(S["dve_dtx"], 1)
            done(sc.activation(ddt, dt, ACT.Abs))
            done(sc.activation(ddt, ddt, ACT.Exp, scale=-1.0))
            sc.activation(ddt, ddt, ACT.Ln, bias=1.0).then_inc(S["act_sp2"], 1)

            act.wait_ge(S["pe_dec"], 1)
            sc.activation(t1, bank(1), ACT.Exp).then_inc(S["act_dec"], 1)
            sc.activation(cd.rearrange("p c i h -> p (c i h)"), PSB[:, 4 * HALF:8 * HALF], ACT.Exp).then_inc(S["act_cd"], 1)

            def conv_start(k):
                act.wait_ge(S["pe_xbc"], k + 1)
                n = XBC_BANK[k]
                done(sc.activation(xc[:, k, :], PSB[:, n * HALF:(n + 2) * HALF], ACT.Identity,
                                   scale=convw[:, k, 3:4], bias=convb[:, k:k + 1]), "act_cv")

            def gate_silu(n):
                act.wait_ge(S["pe_gate"], n + 1)
                sc.activation(sg[:, n // 2, (n % 2) * HALF:(n % 2 + 1) * HALF], bank(n % 2), ACT.Silu)\
                    .then_inc(S["act_gate"], 1)

            conv_start(0)
            conv_start(1)
            for k in range(6):
                if k <= 3:
                    gate_silu(2 * k)
                    gate_silu(2 * k + 1)
                if k + 2 < 6:
                    conv_start(k + 2)
                act.wait_ge(S["dve_cv"], k + 1)
                sc.activation(xc[:, k, :], xc[:, k, :], ACT.Silu).then_inc(S["act_xc"], 1)
            def squares(i):
                act.wait_ge(S["dve_hg"], i + 1)
                tok = slice(i * P, (i + 1) * P)
                sc.activation(xc[:, 0:XT, tok], ya[:, :, tok], ACT.Square).then_inc(S["act_hg2"], 1)

            for i in range(NT):
                if i >= MRING:
                    act.wait_ge(S["pe_yd"], i - MRING + 1)
                for h in range(2):
                    act.wait_ge(S["pe_seg"], 2 * i + h + 1)
                    sc.activation(lm[i % MRING].rearrange("p c h t -> p (c h t)")[:, h * K:(h + 1) * K], PSB[:, 0:2 * HALF],
                                  ACT.Exp).then_inc(S["act_seg"], 1)
                act.wait_ge(S["pe_e"], i + 1)
                if i >= 2:
                    act.wait_ge(S["dve_yo"], i - 1)
                sc.activation(es[i % 2], bank(2), ACT.Exp).then_inc(S["act_e"], 1)
                act.wait_ge(S["pe_tok"], i + 1)
                tok = slice(i * P, (i + 1) * P)
                for k in range(XT):
                    sc.activation(xc[:, k, tok], xc[:, k, tok], ACT.Copy, scale=dskip[:, k:k + 1]).then_inc(S["act_skip"], 1)
                if i >= 3:
                    squares(i - 3)
            squares(NT - 3)
            squares(NT - 2)

            def root_of_half(c):
                act.wait_ge(S["dve_v2"], c + 1)
                sc.activation(hroot[:, 4 * c:4 * c + 4], hms[:, 4 * c:4 * c + 4], ACT.Sqrt).then_inc(S["act_sq2"], 1)

            root_of_half(0)
            squares(NT - 1)
            root_of_half(1)

            def weights_hi(i):
                act.wait_ge(ld_ring[i % RING], 16 * (i // RING + 1))
                if i >= WRING:
                    act.wait_ge(S["pe_dn"], i - WRING + 1)
                sc.activation(wh[:, i % WRING, :], ring[:, i % RING, :], ACT.Copy).then_inc(S["act_wh"], 1)

            weights_hi(0)
            weights_hi(1)
            for c in range(2):
                sigmoid_x(3, c)
                act.wait_ge(S["dve_A"], 7 + c)
                cs = slice(c * HALF, (c + 1) * HALF)
                sc.activation(Ah[:, :, cs], A[:, :, cs], ACT.Copy).then_inc(S["act_ah"], 1)

            def silu(k):
                act.wait_ge(S["pe_up"], k + 1)
                if k >= 4:
                    act.wait_ge(S["dve_hw"], k - 3)
                sc.activation(hs[k % 4], bank(2 * (k % 2)), ACT.Silu).then_inc(S["act_hs"], 1)
                if k % 2 and k // 2 + 2 < MT:
                    weights_hi(k // 2 + 2)

            act.wait_ge(S["dve_lg"], 1)
            sc.activation(pe8[:], lg[:], ACT.Exp).then_inc(S["act_pe"], 1)
            silu(0)
            silu(1)
            act.wait_ge(S["pe_ewb"], 1)
            sc.activation(ewb[:, 0, :], PSB[:, 6 * HALF:8 * HALF], ACT.Copy).then_inc(S["act_ewb"], 1)
            act.wait_ge(S["pe_ewt"], 1)
            sc.activation(ewT, PS[0:NE, 4:6, :].rearrange("p b n -> p (b n)"), ACT.Copy).then_inc(S["act_ewt"], 1)
            for k in range(2, 2 * MT):
                silu(k)

        @block.vector
        def _(dve):
            done = chained(dve, "dve_self")
            v = nc.vector
            dve.wait_ge(ld["f"], 16)
            for ct in range(CT):
                done(v.tensor_scalar(ek[:, ct, :], fT[:, ct, :], 30.0, None, ALU.min), "dve_fmin")
            dve.wait_ge(S["act_exw"], 1)
            dve.wait_ge(S["act_cond"], 1)
            done(v.tensor_scalar(hf[:], tf[:], 0.5, 0.5, ALU.mult, ALU.add))
            done(v.tensor_scalar(cb[:], tf[:], 0.2, 0.8, ALU.mult, ALU.add))
            done(v.tensor_tensor(dec[:], ew[:].unsqueeze(3).broadcast_to([P, 4, CT, B]),
                                 hf[:].unsqueeze(1).unsqueeze(1).broadcast_to([P, 4, CT, B]), ALU.mult))
            done(v.memset(dmat[:, N:N + 1], 0.0))
            dve.wait_ge(ld["small"], 64)

            def tiles(w):
                return w.rearrange("p (a b t) -> p a b t", a=CT, b=B // NCH)

            def inputs(c):
                bs = slice(c * B // NCH, (c + 1) * B // NCH)
                done(v.tensor_tensor(tiles(fc[:, c, :]), tiles(fT[:, c, :]),
                                     cb[:, bs].unsqueeze(1).unsqueeze(3).broadcast_to([P, CT, B // NCH, T]), ALU.mult))
                dve.wait_ge(S["act_ek"], c + 1)
                done(v.tensor_tensor(ekv[:, c, :], ek[:, c, :], fc[:, c, :], ALU.mult), "dve_fc")

            def gate_step(i, k):
                m, c = divmod(i, 2)
                bs = slice(c * B // NCH, (c + 1) * B // NCH)
                g, nf, nb, df, db = sums[i == 1]
                src = ek if k == 1 else ekv
                if k == 0:
                    four = [P, CT, B // NCH, T]
                    done(v.tensor_tensor(tiles(dmat[:, 0:N]), dec[:, m, :, bs].unsqueeze(3).broadcast_to(four),
                                         notfirst[:].unsqueeze(1).unsqueeze(1).broadcast_to(four), ALU.mult))
                if k in (1, 2):
                    fwd, bwd = (df, db) if k == 1 else (nf, nb)
                    done(v.tensor_tensor_scan(fwd, dmat[:, 0:N], src[:, c, :], 0.0, ALU.mult, ALU.add))
                    done(v.tensor_tensor_scan(bwd[:, ::-1], dmat[:, 1:N + 1][:, ::-1], src[:, c, ::-1], 0.0,
                                              ALU.mult, ALU.add), "dve_scan")
                if k == 2:
                    dve.wait_ge(S["act_euk"], CT * (i + 1))
                    done(v.scalar_tensor_tensor(g, g, E30, ek[:, c, :], ALU.min, ALU.subtract), "dve_g")
                if k == 3:
                    done(v.tensor_tensor(nf, nf, nb, ALU.add), "dve_nf")
                if k == 4:
                    dve.wait_ge(S["pool_den"], i + 1)
                    done(v.tensor_scalar(df, df, 1e-8, None, ALU.max), "dve_den")
                if k == 5:
                    dve.wait_ge(S["act_guess"], i + 1)
                    done(v.tensor_tensor(df, df, db, ALU.mult))
                    done(v.scalar_tensor_tensor(df, df, 2.0, db, ALU.subtract, ALU.mult))
                if k == 6:
                    dve.wait_ge(S["pool_num"], i + 1)
                    done(v.scalar_tensor_tensor(R[:, m, c, :], nf, -1.0, df, ALU.mult, ALU.mult), "dve_R")

            def gate(m, c):
                dve.wait_ge(S["act_sg"], 2 * m + c + 1)
                a_ = A[:, :, c * HALF:(c + 1) * HALF]
                done(v.tensor_tensor(a_, a_, R[:, m, c, :].rearrange("p (a n) -> p a n", a=CT), ALU.mult), "dve_A")

            def ternary_scales():
                dve.wait_ge(S["pe_wsum"], 1)
                done(v.tensor_scalar(wsc[:], bank(6, 3), 1.0 / (D * H), None, ALU.mult))
                done(v.tensor_scalar(winv[:], wsc[:], 1e-8, None, ALU.add))
                done(v.reciprocal(winv[:], winv[:]), "dve_winv")
                done(v.tensor_scalar(wtmp[:], wsc[:], -1.0, 1.0, ALU.mult, ALU.add))
                done(v.reciprocal(wtmp[:], wtmp[:]))
                done(v.tensor_scalar(wsc[:], wsc[:], 1.0, None, ALU.add))
                done(v.tensor_tensor(wtmp[:], wtmp[:], wsc[:], ALU.mult), "dve_ln")

            def keys_values(c):
                for mt in range(CT):
                    dve.wait_ge(S["pe_k"], CT * c + mt + 1)
                    done(v.tensor_copy(kT[:, mt, c * HALF:(c + 1) * HALF], bank(2 + mt)), "dve_k")
                for i in range(4 * c, 4 * c + 4):
                    dve.wait_ge(S["pe_v"], i + 1)
                    done(v.tensor_copy(vv[:, i, :, 0:HD], bank(4 + i % 4, D).rearrange("p (h d) -> p h d", h=NH)), "dve_v")

            inputs(0)
            for k in range(4):
                gate_step(0, k)
            inputs(1)
            gate_step(0, 4)
            for k in range(2):
                gate_step(1, k)
            ternary_scales()
            gate_step(1, 2)
            gate_step(0, 5)
            gate_step(0, 6)
            gate(0, 0)
            gate_step(1, 3)
            gate_step(1, 4)
            gate_step(1, 5)
            gate_step(1, 6)
            gate(0, 1)
            keys_values(0)

            def ternary(w):
                dve.wait_ge(S["act_tanh"], w + 1)
                done(v.tensor_scalar(wter[:, w, :], R[:, 1 + w].rearrange("p c n -> p (c n)"), MAGIC, MAGIC,
                                     ALU.add, ALU.subtract), "dve_tern")

            done(v.memset(vv[:, :, :, HD:VW], 1.0))
            dve.wait_ge(ld["const"], 6 * 16)
            done(v.tensor_copy(identb[:], ident[:]))
            done(v.tensor_copy(negmask[:], negmaskf))
            keys_values(1)
            def add_attention(i):
                dve.wait_ge(S["pe_wo"], i + 1)
                sl = xT[:, :, i * P:(i + 1) * P]
                done(v.tensor_tensor(sl, sl, PS[:, 7, 256:512].rearrange("p (a n) -> p a n", a=CT), ALU.add), "dve_x")

            def normalise(i):
                dve.wait_ge(S["pe_z"], 4 * (i + 1))
                zp = PS[:, 6, 0:NH * VW].rearrange("p (h d) -> p h d", h=NH)
                done(v.reciprocal(rinv[:, i % 2, :], zp[:, :, HD]))
                if i >= 2:
                    dve.wait_ge(S["pe_zt"], i - 1)
                done(v.tensor_tensor(zn[i % 2].rearrange("p (h d) -> p h d", h=NH), zp[:, :, 0:HD],
                                     rinv[:, i % 2, :].unsqueeze(2).broadcast_to([P, NH, HD]), ALU.mult), "dve_zn")

            for u in range(32):
                tt = (u // 4) % 2
                if u % 4 == 2 and u >= 4:
                    normalise(u // 4 - 1)
                dve.wait_ge(S["pe_sc"], u + 1)
                if u >= 2:
                    dve.wait_ge(S["act_exp"], 4 * (u - 1))
                src = PSB[:, 2 * (u % 2) * HALF:(2 * (u % 2) + 2) * HALF].rearrange("p (j s) -> p j s", j=4)
                done(v.tensor_reduce(nmx[:, u % 2, :], src[:, :, 0:P * (tt + 1)], X, ALU.max, negate=True), "dve_max")
                if u in (1, 2, 3):
                    ternary(u - 1)
                if u % 4 == 1 and u >= 8:
                    add_attention(u // 4 - 2)
                i, k = divmod(u, FRAME)
                if k < 2 and i:
                    gate_step(i + 1, FRAME + k)
                if i < 6:
                    gate_step(i + 2, k)
            add_attention(6)
            normalise(7)

            def add_x(psum, mt, ch, name):
                sl = xT[:, mt, ch * HALF:(ch + 1) * HALF]
                done(v.tensor_tensor(sl, sl, psum, ALU.add), name)

            add_attention(NT - 1)

            dve.wait_ge(S["act_atanh"], 1)
            done(v.tensor_scalar(wat[:], wat[:], 0.5 / 127.0, None, ALU.mult))
            gate(1, 0)
            gate(1, 1)
            dve.wait_ge(ld["gb"], 16)

            def round_clip(dst, w, name):
                done(v.tensor_scalar(w, w, 127.0, -128.0, ALU.min, ALU.max))
                done(v.tensor_scalar(dst, w, MAGIC, MAGIC, ALU.add, ALU.subtract), name)

            for c in range(2):
                dve.wait_ge(S["act_atok"], c + 1)
                done(v.tensor_tensor(zz[c][0], atok[c], gb[:, 0:D].unsqueeze(1).broadcast_to([P, 4, D]), ALU.mult))
                done(v.tensor_reduce(peak[:, 0, 4 * c:4 * c + 4], zz[c][0], X, ALU.max, apply_absolute_value=True))
            dve.wait_ge(S["act_ss"], NT)
            done(v.tensor_scalar(msq[:], ss[:], 1.0 / D, 1e-8, ALU.mult, ALU.add), "dve_var")
            for c in range(2):
                dve.wait_ge(S["pool_z2"], c + 1)
                done(v.tensor_reduce(peak[:, 1, 4 * c:4 * c + 4], zz[c][1], X, ALU.max, apply_absolute_value=True))
            pair = [P, 2, NT]
            dve.wait_ge(S["act_sqrt"], 1)
            done(v.reciprocal(rms1[:], root[:]))
            r1 = rms1[:].unsqueeze(1).broadcast_to(pair)
            done(v.tensor_tensor(peak[:], peak[:], r1, ALU.mult))
            done(v.tensor_scalar(peak[:], peak[:], 1e-4, None, ALU.max))
            done(v.reciprocal(ipeak[:], peak[:]))
            done(v.scalar_tensor_tensor(iscale[:], ipeak[:], 127.0, r1, ALU.mult, ALU.mult), "dve_scale")
            done(v.tensor_tensor(oscale[:], peak[:], wat[:, 0:2].unsqueeze(2).broadcast_to(pair), ALU.mult))
            for c in range(2):
                done(v.tensor_tensor(zs[c][0], zz[c][0], iscale[:, 0, 4 * c:4 * c + 4].unsqueeze(2).broadcast_to([P, 4, D]),
                                     ALU.mult))
                for l in range(2):
                    if l == 1:
                        dve.wait_ge(S["pool_zs"], c + 1)
                    round_clip(xqb[c][l], zs[c][l], "dve_xq")

            def add_tok(i):
                dve.wait_ge(S["pe_ot"], i + 1)
                sl = xT[:, :, i * P:(i + 1) * P]
                done(v.tensor_tensor(sl, sl, PS[:, 5, 0:256].rearrange("p (a n) -> p a n", a=2), ALU.add), "dve_x")

            for s in range(2 * NT):
                if s < NT:
                    if s >= 2:
                        dve.wait_ge(S["pool_z3"], s - 1)
                        dve.wait_ge(S["act_ss3"], s - 1)
                    for k in (2 * s, 2 * s + 1):
                        dve.wait_ge(S["act_sw"], k + 1)
                        done(v.scalar_tensor_tensor(hh[s % 2][:, (k % 2) * HALF:(k % 2 + 1) * HALF], bank(2 * (k % 2) + 1),
                                                    oscale[:, 1, s:s + 1], sw[k % 2], ALU.mult, ALU.mult), "dve_h")
                if 1 <= s <= NT:
                    dve.wait_ge(S["pool_z3"], s)
                    done(v.tensor_reduce(peak3[:, s - 1:s], z3[:, s - 1, :], X, ALU.max, apply_absolute_value=True))
                if s in (4, 8):
                    c = s // 4 - 1
                    t = slice(4 * c, 4 * c + 4)
                    dve.wait_ge(S["act_ss3"], s)
                    done(v.tensor_scalar(msq3[:, t], ss3[:, t], 1.0 / H, 1e-8, ALU.mult, ALU.add), "dve_var3")
                    dve.wait_ge(S["act_sqrt3"], c + 1)
                    done(v.reciprocal(rms3[:, t], root3[:, t]))
                    done(v.tensor_tensor(peak3[:, t], peak3[:, t], rms3[:, t], ALU.mult))
                    done(v.tensor_scalar(peak3[:, t], peak3[:, t], 1e-4, None, ALU.max))
                    done(v.tensor_scalar(oscale3[:, t], peak3[:, t], wat[:, 2:3], None, ALU.mult))
                    done(v.reciprocal(iscale3[:, t], peak3[:, t]))
                    done(v.scalar_tensor_tensor(iscale3[:, t], iscale3[:, t], 127.0, rms3[:, t], ALU.mult, ALU.mult), "dve_scale3")
                if 0 <= s - 8:
                    add_tok(s - 8)
                if 0 <= s - 5 < NT:
                    i = s - 5
                    dve.wait_ge(S["act_y3"], i + 1)
                    if i >= 2:
                        dve.wait_ge(S["pe_hqt"], i - 1)
                    round_clip(hq[i % 2], y3[i % 2], "dve_hq")
                if s == 13:
                    gate(2, 0)

            gate(2, 1)
            dve.wait_ge(ld["ssd"], 160)
            dve.wait_ge(S["act_exw"], 2)
            done(v.tensor_scalar(anegb[:], anegb[:], -1.0, None, ALU.mult))
            done(v.tensor_scalar(anegj[:], anegj[:], -1.0, None, ALU.mult))
            dve.wait_ge(S["pe_dt"], 1)
            done(v.tensor_tensor(dt, bank(0).rearrange("p (i h) -> p i h", i=NT),
                                 dtb[:].unsqueeze(1).broadcast_to([P, NT, SH]), ALU.add), "dve_dtx")
            dve.wait_ge(S["act_sp2"], 1)
            done(v.scalar_tensor_tensor(dt, dt, 0.0, ddt, ALU.max, ALU.add))
            done(v.tensor_tensor(dA, dt, anegb[:].unsqueeze(1).broadcast_to([P, NT, SH]), ALU.mult), "dve_dt")
            for k in range(6):
                dve.wait_ge(S["act_cv"], k + 1)
                o = xc[:, k, :].rearrange("p (b t) -> p b t", b=B)
                n = XBC_BANK[k]
                s = PSB[:, n * HALF:(n + 2) * HALF].rearrange("p (b t) -> p b t", b=B)
                for back in (1, 2, 3):
                    done(v.scalar_tensor_tensor(o[:, :, back:], s[:, :, 0:T - back], convw[:, k, 3 - back:4 - back],
                                                o[:, :, back:], ALU.mult, ALU.add), "dve_cv" if back == 3 else "dve_self")
                if k == 0:
                    dve.wait_ge(S["act_dec"], 1)
                    done(v.tensor_tensor(ddt, dt, t1.rearrange("p (i h) -> p i h", i=NT), ALU.mult), "dve_ddt")
                if k < 2:
                    for j in (2 * k, 2 * k + 1):
                        for c in range(NC):
                            done(v.tensor_copy(dtj[Q * j:Q * j + Q, :, c, :], dt[Q * c:Q * c + Q, :, HG * j:HG * (j + 1)]))
                if k == 1:
                    done(v.tensor_tensor(dAj.rearrange("p i c h -> p (i c) h"), dtj.rearrange("p i c h -> p (i c) h"),
                                         anegj[:].unsqueeze(1).broadcast_to([P, NT * NC, HG]), ALU.mult), "dve_dt")
            dve.wait_ge(S["act_cd"], 1)

            def nat(w):
                return w.rearrange("p (j h) -> p h j", j=4).unsqueeze(3).broadcast_to([P, HG, 4, SP_])

            def hjp(w):
                return w.rearrange("p (h j q) -> p h j q", h=HG, j=4)

            def front(i, part):
                xt = bank(4)
                if part == 0:
                    dve.wait_ge(S["pe_tok"], i + 1)
                    done(v.tensor_tensor(btok[i % 2], bank(5, P).unsqueeze(1).broadcast_to([P, NC, P]), cones[:], ALU.mult))
                    done(v.tensor_tensor(hjp(xdd[i % 2]), hjp(xt), nat(ddt[:, i, :]), ALU.mult), "dve_tok")
                    if i >= 1:
                        dve.wait_ge(S["pool_m"], i)
                    done(v.tensor_tensor(gm, PS[:, 5, 128:256].rearrange("p (c t) -> p c t", c=NC),
                                         step[:].unsqueeze(1).broadcast_to([P, NC, Q]), ALU.mult), "dve_gm")
                    if i < MRING:
                        dve.wait_ge(S["pool_zero"], i + 1)
                    else:
                        dve.wait_ge(S["pe_yd"], i - MRING + 1)
                j = part
                for c in range(NC):
                    done(v.tensor_tensor(xbd[i % MRING][Q * j:Q * j + Q, c, :, j, :],
                                         hjp(xt)[Q * c:Q * c + Q, :, j, :],
                                         dtj[Q * j:Q * j + Q, i, c, :].unsqueeze(2).broadcast_to([Q, HG, SP_]),
                                         ALU.mult), "dve_xbd" if (j, c) == (3, 3) else "dve_self")

            def state(i, c):
                if i % 2 == 1 and c == NC - 1:
                    return
                n = (c + 1) % 2
                dve.wait_ge(S["pe_sl"], 7 * (i // 2) + 4 * (i % 2) + c + 1)
                done(v.tensor_tensor(hjp(st[n]), hjp(st[1 - n]), nat(cd[:, c, i, :]), ALU.mult))
                done(v.tensor_tensor(st[n], st[n], bank(7), ALU.add), "dve_s")

            def norm_of_half(c):
                t = slice(4 * c, 4 * c + 4)
                dve.wait_ge(S["pe_var"], 4 * c + 4)
                done(v.tensor_scalar(hms[:, t], bank(c, 4), 1.0 / DIN, 1e-5, ALU.mult, ALU.add), "dve_v2")
                dve.wait_ge(S["act_sq2"], c + 1)
                done(v.reciprocal(hrms[:, t], hroot[:, t]), "dve_rs")

            def gated(i):
                yt = ya[:, :, i * P:(i + 1) * P]
                dve.wait_ge(S["pe_yd"], i + 1)
                done(v.tensor_tensor(yt, yo[i % 2].rearrange("p (a n) -> p a n", a=XT),
                                     bank(6).rearrange("p (a n) -> p a n", a=XT), ALU.add), "dve_y")
                dve.wait_ge(S["act_skip"], 4 * (i + 1))
                done(v.tensor_tensor(yt, yt, xc[:, 0:XT, i * P:(i + 1) * P], ALU.add))
                done(v.tensor_tensor(yt, yt, sg[:, :, i * P:(i + 1) * P], ALU.mult), "dve_hg")

            done(v.memset(st[0], 0.0), "dve_s")
            for part in range(4):
                front(0, part)
            for i in range(NT):
                for c in range(NC):
                    state(i, c)
                    if i % 2 and c == NC - 1 and i + 1 < NT:
                        dve.wait_ge(S["pe_yo"], 4 * i + 3)
                        done(v.memset(st[0], 0.0), "dve_s")
                    if i + 1 < NT:
                        front(i + 1, c)
                    if c == 0 and i >= 2:
                        gated(i - 2)
                dve.wait_ge(S["pe_yo"], 4 * (i + 1))
                dve.wait_ge(S["act_e"], i + 1)
                done(v.tensor_tensor(yo[i % 2], es[i % 2], bank(3), ALU.mult), "dve_yo")
            gated(NT - 2)
            norm_of_half(0)
            gated(NT - 1)

            def finish(ch):
                dve.wait_ge(S["pe_rsb"], ch + 1)
                done(v.tensor_copy(rsb, bank(7 - ch)))
                for mt in range(CT):
                    k = 2 * ch + mt
                    dve.wait_ge(S["pe_op"], k + 1)
                    done(v.tensor_tensor(t1, bank((2, 4, 5, 3)[k]), rsb, ALU.mult))
                    add_x(t1, mt, ch, "dve_x")

            def split_input(c):
                dve.wait_ge(S["act_ah"], c + 1)
                cs = slice(c * HALF, (c + 1) * HALF)
                done(v.tensor_tensor(Al[:, :, cs], A[:, :, cs], Ah[:, :, cs], ALU.subtract), "dve_al")

            finish(0)
            norm_of_half(1)
            gate(3, 0)
            split_input(0)
            finish(1)
            gate(3, 1)
            split_input(1)
            dve.wait_ge(S["pe_lg"], NT)
            lp = bank(4, NT * NE).rearrange("p (i e) -> p i e", i=NT)
            done(v.tensor_reduce(mx8[:], lp, X, ALU.max))
            b8e = [P, NT, NE]
            done(v.tensor_tensor(lg[:], lp, mx8[:].unsqueeze(2).broadcast_to(b8e), ALU.subtract), "dve_lg")
            dve.wait_ge(S["act_pe"], 1)
            for i in range(NT):
                done(v.max(top[:, i, :], pe8[:, i, :]))
                done(v.max_index(tix[:, i, :], top[:, i, :], pe8[:, i, :]))
            done(v.tensor_copy(tixf[:], tix[:]))
            done(v.tensor_tensor(mx8[:], top[:, :, 0], top[:, :, 1], ALU.add))
            done(v.reciprocal(mx8[:], mx8[:]))
            done(v.tensor_tensor(lg[:], top[:], mx8[:].unsqueeze(2).broadcast_to(b8e), ALU.mult))
            io = iota[:].unsqueeze(1).broadcast_to(b8e)
            for s in range(2):
                dst = ewt if s == 0 else ewm
                done(v.tensor_tensor(dst[:], io, tixf[:, :, s:s + 1].broadcast_to(b8e), ALU.is_equal))
                done(v.tensor_tensor(dst[:], dst[:], lg[:, :, s:s + 1].broadcast_to(b8e), ALU.mult))
            done(v.tensor_tensor(ewt[:], ewt[:], ewm[:], ALU.add), "dve_ew")

            def product(k):
                dve.wait_ge(S["act_hs"], k + 1)
                done(v.tensor_tensor(hs[k % 4], hs[k % 4], bank(2 * (k % 2) + 1), ALU.mult), "dve_up")

            def weighted(k):
                i, ch = divmod(k, 2)
                first, last = i * P // FF, (i * P + P - 1) // FF
                if k == 0:
                    dve.wait_ge(S["act_ewb"], 1)
                elif ch == 0 and last:
                    dve.wait_ge(ld_ewb[last], 16)
                if k >= 2:
                    dve.wait_ge(S["pool_hl"], k - 1)
                cols = slice(ch * HALF, (ch + 1) * HALF)
                cut = (last * FF - i * P) if first != last else P
                if first != last:
                    done(v.tensor_tensor(hw[k % 2][cut:P, :], hs[k % 4][cut:P, :], ewb[cut:P, last, cols], ALU.mult))
                done(v.tensor_tensor(hw[k % 2][0:cut, :], hs[k % 4][0:cut, :], ewb[0:cut, first, cols], ALU.mult), "dve_hw")
                if k >= 4:
                    dve.wait_ge(S["pe_dn"], (k - 4) // 2 + 1)
                done(v.tensor_copy(hwh[:, k % 4, :], hw[k % 2]), "dve_hh")

            for k in range(2 * MT):
                product(k)
                weighted(k)
            for k in range(4):
                dve.wait_ge(S["pe_dn"], MT)
                add_x(bank(4 + k), k // 2, k % 2, "dve_out")

        @block.tensor
        def _(pe):
            mm = nc.tensor.matmul

            def acc(dst, pairs, name=None):
                for n, (l, r) in enumerate(pairs):
                    last = mm(dst, l, r, start=(n == 0), stop=(n == len(pairs) - 1))
                if name:
                    last.then_inc(S[name], 1)
                return last

            pe.wait_ge(ld["small"], 64)
            acc(bank(7, B), [(ones[0:64, :], condT[:, :])], "pe_cond")
            pe.wait_ge(S["act_wabs"], 3)
            acc(bank(6, 3), [(ones[:], wabs[:])], "pe_wsum")

            pe.wait_ge(ld["attn"], 32)
            pe.wait_ge(ld["const"], 6 * 16)
            for ch in range(NCH):
                pe.wait_ge(S["dve_A"], ch + 1)
                for mt in range(CT):
                    for qk in range(2):
                        if ch:
                            pe.wait_ge(S["act_q" if qk == 0 else "dve_k"], mt + 1)
                        acc(bank(2 * qk + mt), [(wqkvo[:, qk, kt, mt * P:(mt + 1) * P], A[:, kt, ch * HALF:(ch + 1) * HALF])
                                                for kt in range(CT)], "pe_q" if qk == 0 else "pe_k")
                pe.wait_ge(S["act_cond"], 1)
                pe.wait_ge(S["dve_winv"], 1)
                for i in range(4 * ch, 4 * ch + 4):
                    if ch:
                        pe.wait_ge(S["dve_v"], i - 3)
                    acc(bank(4 + i % 4, D), [(A[:, kt, i * P:(i + 1) * P], wqkvo[:, 2, kt, :]) for kt in range(CT)], "pe_v")

            def scores(u):
                i, g = divmod(u, 4)
                b, tt = divmod(i, 2)
                n = P * (tt + 1)
                if u >= 2:
                    pe.wait_ge(S["act_exp"], 4 * (u - 1))
                pe.wait_ge(S["pool_qm"], u + 1)
                for j in range(4):
                    o = PS[:, 2 * (u % 2) + j // 2, (j % 2) * 256:(j % 2) * 256 + n]
                    mm(o, qm[u % QRING][:, j, :], kT[:, g // 2, b * T:b * T + n], start=True, stop=False)
                    last = mm(o[:, tt * P:n], identb[:], negmask[:], start=False, stop=True)
                last.then_inc(S["pe_sc"], 1)

            def turn(u):
                tt = (u // 4) % 2
                pe.wait_ge(S["act_exp"], 4 * (u + 1))
                if u >= 1:
                    pe.wait_ge(S["act_pt"], u)
                for j in range(4):
                    for k in range(tt + 1):
                        c = (j * (tt + 1) + k) * P
                        last = nc.tensor.transpose(PSB[:, 4 * HALF + c:4 * HALF + c + P],
                                                   pr[u % 2][:, j, k * P:(k + 1) * P], ident[:])
                last.then_inc(S["pe_pt"], 1)

            def values(u):
                i, g = divmod(u, 4)
                b, tt = divmod(i, 2)
                pe.wait_ge(S["act_pt"], u + 1)
                if g == 0 and i >= 1:
                    pe.wait_ge(S["dve_zn"], i)
                for j in range(4):
                    h = 4 * g + j
                    last = acc(PS[:, 6, h * VW:(h + 1) * VW],
                               [(pt[u % 2][:, (j * (tt + 1) + k) * P:(j * (tt + 1) + k + 1) * P],
                                 vv[:, 2 * b + k, h, :]) for k in range(tt + 1)])
                last.then_inc(S["pe_z"], 1)

            def turn_z(i):
                pe.wait_ge(S["dve_zn"], i + 1)
                if i >= 1:
                    pe.wait_ge(S["dve_x"], i)
                for ct in range(CT):
                    last = nc.tensor.transpose(PS[:, 7, ct * P:(ct + 1) * P], zn[i % 2][:, ct * P:(ct + 1) * P], ident[:])
                last.then_inc(S["pe_zt"], 1)

            def project(i):
                pe.wait_ge(S["act_zt"], i + 1)
                for mt in range(CT):
                    last = acc(PS[:, 7, 256 + mt * P:256 + (mt + 1) * P],
                               [(wqkvo[:, 3, kt, mt * P:(mt + 1) * P], zT[:, kt, i * P:(i + 1) * P]) for kt in range(CT)])
                last.then_inc(S["pe_wo"], 1)

            pe.wait_ge(S["act_q"], 4)
            pe.wait_ge(S["dve_k"], 4)
            pe.wait_ge(S["dve_v"], 8)
            for u in range(34):
                if u < 32:
                    scores(u)
                if 1 <= u < 33:
                    turn(u - 1)
                if u >= 2:
                    values(u - 2)
                if u >= 6 and u % 4 == 2:
                    turn_z(u // 4 - 1)
                if u >= 6 and u % 4 == 0:
                    project(u // 4 - 2)
            turn_z(7)
            project(7)

            def turn_in(c):
                pe.wait_ge(S["dve_A"], 3 + c)
                for i in range(4):
                    for ct in range(CT):
                        n = (6 - 2 * c) * HALF + i * D + ct * P
                        last = nc.tensor.transpose(PSB[:, n:n + P],
                                                   A[:, ct, (4 * c + i) * P:(4 * c + i + 1) * P], ident[:])
                last.then_inc(S["pe_at"], 1)

            def turn_back(c):
                pe.wait_ge(S["act_atok"], c + 1)
                for l in range(2):
                    pe.wait_ge(S["dve_xq"], 2 * c + l + 1)
                    o = PS[:, 6 - 2 * c + l, :].bitcast(BF)
                    for ct in range(CT):
                        for i in range(4):
                            last = nc.tensor.transpose(o[:, ct * HALF + i * P:ct * HALF + (i + 1) * P],
                                                       xqb[c][l][:, i, ct * P:(ct + 1) * P], identb[:])
                    last.then_inc(S["pe_xqt"], 1)

            def hidden(k):
                i, half = divmod(k, 2)
                if k >= 2:
                    pe.wait_ge(S["dve_h"], k - 1)
                for l in range(2):
                    last = acc(bank(2 * (k % 2) + l),
                               [(xqT[l][:, ct, i * P:(i + 1) * P], wter[:, l, ct * H + half * HALF:ct * H + (half + 1) * HALF])
                                for ct in range(CT)])
                last.then_inc(S["pe_h"], 1)

            turn_in(0)
            turn_in(1)
            turn_back(0)
            turn_back(1)
            pe.wait_ge(S["dve_tern"], 3)
            pe.wait_ge(S["act_xqt"], 2)
            pe.wait_ge(S["dve_x"], X_ATT)
            for s in range(2 * NT):
                if s < NT:
                    if s == 4:
                        pe.wait_ge(S["act_xqt"], 4)
                    hidden(2 * s)
                    hidden(2 * s + 1)
                if 0 <= s - 7 < NT:
                    i = s - 7
                    pe.wait_ge(S["act_o"], i + 1)
                    if i:
                        pe.wait_ge(S["dve_x"], X_ATT + i)
                    for ct in range(CT):
                        last = nc.tensor.transpose(PS[:, 5, ct * P:(ct + 1) * P], otok[i % 2][:, ct * P:(ct + 1) * P], ident[:])
                    last.then_inc(S["pe_ot"], 1)
                if 0 <= s - 6 < NT:
                    i = s - 6
                    pe.wait_ge(S["act_hqt"], i + 1)
                    if i:
                        pe.wait_ge(S["act_o"], i)
                    acc(bank(4, D), [(hqT[i % 2][:, k, :], wter[:, 2, k * D:(k + 1) * D]) for k in range(HT)], "pe_o")
                if 0 <= s - 5 < NT:
                    i = s - 5
                    pe.wait_ge(S["dve_hq"], i + 1)
                    if i >= 2:
                        pe.wait_ge(S["act_hqt"], i - 1)
                    o = PS[:, 6 + i % 2, :].bitcast(BF)
                    for k in range(HT):
                        last = nc.tensor.transpose(o[:, k * P:(k + 1) * P], hq[i % 2][:, k * P:(k + 1) * P], identb[:])
                    last.then_inc(S["pe_hqt"], 1)

            pe.wait_ge(ld["ssd"], 160)
            pe.wait_ge(S["dve_A"], 6)
            for i in range(NT):
                last = acc(PS[:, 0, i * SH:(i + 1) * SH], [(A[:, kt, i * P:(i + 1) * P], inproj[:, kt, PROJ - SH:PROJ])
                                                           for kt in range(CT)])
            last.then_inc(S["pe_dt"], 1)

            def conv_in(k):
                c0 = DIN + k * P
                for ch in range(NCH):
                    last = acc(bank(XBC_BANK[k] + ch), [(inproj[:, kt, c0:c0 + P], A[:, kt, ch * HALF:(ch + 1) * HALF])
                                                        for kt in range(CT)])
                last.then_inc(S["pe_xbc"], 1)

            def gate_in(n):
                mt, ch = divmod(n, 2)
                if n >= 2:
                    pe.wait_ge(S["act_gate"], n - 1)
                acc(bank(ch), [(inproj[:, kt, mt * P:(mt + 1) * P], A[:, kt, ch * HALF:(ch + 1) * HALF])
                               for kt in range(CT)], "pe_gate")

            conv_in(0)
            pe.wait_ge(S["dve_dt"], 1)
            dAf = dA.rearrange("p i h -> p (i h)")
            acc(bank(1), [(ugt[:], dAf)])
            pe.wait_ge(ld["cones"], 16)
            for c in range(NC):
                last = acc(bank(4 + c), [(cones[:, c, :], dAf)])
            last.then_inc(S["pe_dec"], 1)
            pe.wait_ge(S["act_dec"], 1)
            pe.wait_ge(S["act_cd"], 1)
            for k in range(1, 6):
                if k >= 3:
                    pe.wait_ge(S["dve_cv"], k - 2)
                conv_in(k)
                if k < 5:
                    gate_in(2 * k - 2)
                    gate_in(2 * k - 1)
            pe.wait_ge(S["act_gate"], 8)
            pe.wait_ge(S["dve_cv"], 4)

            def front(i, part):
                tok = slice(i * P, (i + 1) * P)
                if part == 0:
                    if i:
                        pe.wait_ge(S["dve_xbd"], i)
                        pe.wait_ge(S["dve_gm"], i)
                    for k in range(XT):
                        nc.tensor.transpose(PS[:, 4, k * P:(k + 1) * P], xc[:, k, tok], ident[:])
                    nc.tensor.transpose(PS[:, 5, 0:P], xc[:, 4, tok], ident[:])
                    for c in range(NC):
                        cs = slice(i * P + c * Q, i * P + (c + 1) * Q)
                        for j in range(4):
                            last = acc(PS[Q * j:Q * j + Q, 5, 128 + c * Q:128 + (c + 1) * Q], [(xc[:, 4, cs], xc[:, 5, cs])])
                    last.then_inc(S["pe_tok"], 1)
                elif part < 3:
                    pe.wait_ge(S["pool_stp"], i + 1)
                    if 2 * i + part - 1:
                        pe.wait_ge(S["act_seg"], 2 * i + part - 1)
                    for h in range(2):
                        last = acc(bank(h), [(ugt[:], stp[:, 2 * (part - 1) + h, :, :].rearrange("p h t -> p (h t)"))])
                    last.then_inc(S["pe_seg"], 1)
                else:
                    pe.wait_ge(S["pool_dae"], i + 1)
                    if i:
                        pe.wait_ge(S["act_e"], i)
                    for k in range(XT):
                        last = acc(PS[:, 2, k * P:(k + 1) * P], [(dAe[:, k * P:(k + 1) * P], tri[:])])
                    last.then_inc(S["pe_e"], 1)

            def within(i, c):
                if c == 0:
                    pe.wait_ge(S["dve_xbd"], i + 1)
                    pe.wait_ge(S["pool_m"], i + 1)
                    if i:
                        pe.wait_ge(S["dve_y"], i)
                for h in range(HG):
                    last = acc(PS[Q * (h % 4):Q * (h % 4) + Q, 6, (h // 4) * P + c * Q:(h // 4) * P + (c + 1) * Q],
                               [(xbd[i % MRING][:, c, h, :, :].rearrange("p j q -> p (j q)"), lm[i % MRING][:, c, h, :])])
                if c == NC - 1:
                    last.then_inc(S["pe_yd"], 1)

            def mean_square(i):
                pe.wait_ge(S["act_hg2"], i + 1)
                if i == 0:
                    pe.wait_ge(S["act_seg"], 2 * NT)
                acc(PS[:, i // 4, i % 4:i % 4 + 1], [(xc[:, k, i * P:(i + 1) * P], ones[:, 0:1]) for k in range(XT)], "pe_var")

            def spread_rms(c):
                pe.wait_ge(S["dve_rs"], c + 1)
                pe.wait_ge(S["dve_y"], NT)
                for i in range(4):
                    last = mm(PS[:, 7 - c, i * P:(i + 1) * P], hrms[:, 4 * c + i:4 * c + i + 1].broadcast_to([P, P]), ident[:],
                              start=True, stop=True)
                last.then_inc(S["pe_rsb"], 1)

            def output(k):
                ch, mt = divmod(k, 2)
                b = (2, 4, 5, 3)[k]
                if k == 0:
                    pe.wait_ge(S["act_e"], NT)
                    pe.wait_ge(S["act_opw"], XT)
                    pe.wait_ge(S["dve_hg"], 4)
                if k == 1:
                    pe.wait_ge(S["dve_xbd"], NT)
                if k == 2:
                    pe.wait_ge(S["dve_hg"], NT)
                acc(bank(b), [(outproj[:, kt, mt * P:(mt + 1) * P], ya[:, kt, ch * HALF:(ch + 1) * HALF])
                              for kt in range(XT)], "pe_op")

            front(0, 1)
            front(0, 3)
            pe.wait_ge(S["act_xc"], 6)
            front(0, 0)
            front(0, 2)
            for i in range(NT):
                for c in range(NC):
                    if c == 0 and i >= 2:
                        within(i - 2, NC - 1)
                    if i + 1 < NT:
                        front(i + 1, c)
                    pe.wait_ge(S["dve_tok"], i + 1)
                    pe.wait_ge(S["dve_s"], 8 * (i // 2) + 4 * (i % 2) + c + 1)
                    if i and c == 0:
                        pe.wait_ge(S["dve_yo"], i)
                    cs = slice(i * P + c * Q, i * P + (c + 1) * Q)
                    if not (i % 2 == 1 and c == NC - 1):
                        acc(bank(7), [(btok[i % 2][:, c, :], xdd[i % 2])], "pe_sl")
                    for k in range(XT):
                        last = acc(PS[:, 3, k * P + c * Q:k * P + (c + 1) * Q],
                                   [(st[c % 2][:, k * P:(k + 1) * P], xc[:, 5, cs])])
                    last.then_inc(S["pe_yo"], 1)
                    if i and c:
                        within(i - 1, c - 1)
            within(NT - 2, NC - 1)
            for t in range(4):
                mean_square(t)
            for c in range(NC):
                within(NT - 1, c)
            output(0)
            spread_rms(0)
            for t in range(4, NT - 1):
                mean_square(t)
            output(1)
            mean_square(NT - 1)
            output(2)
            spread_rms(1)
            output(3)

            def down(i):
                pe.wait_ge(S["dve_hh"], 2 * i + 2)
                pe.wait_ge(S["pool_hl"], 2 * i + 2)
                for mt in range(CT):
                    cols = slice(512 + mt * P, 512 + (mt + 1) * P)
                    for n, (w, h) in enumerate(((wh, hwh), (wh, hwl), (wl, hwh))):
                        for ch in range(NCH):
                            last = mm(bank(4 + 2 * mt + ch), w[:, i % WRING, cols], h[:, (2 * i + ch) % 4, :],
                                      start=(i == 0 and n == 0), stop=(i == MT - 1 and n == 2))
                last.then_inc(S["pe_dn"], 1)

            def up(k):
                i, ch = divmod(k, 2)
                pe.wait_ge(S["act_wh"], i + 1)
                pe.wait_ge(S["pool_wl"], i + 1)
                t = slice(ch * HALF, (ch + 1) * HALF)
                if k < 2:
                    pe.wait_ge(S["act_ah"], k + 1)
                    pe.wait_ge(S["dve_al"], k + 1)
                else:
                    pe.wait_ge(S["dve_up"], k - 1)
                for w in range(2):
                    pairs = []
                    for kt in range(CT):
                        cols = slice(w * 256 + kt * P, w * 256 + (kt + 1) * P)
                        hi, lo = wh[:, i % WRING, cols], wl[:, i % WRING, cols]
                        pairs += [(hi, Ah[:, kt, t]), (hi, Al[:, kt, t]), (lo, Ah[:, kt, t])]
                    last = acc(bank(2 * (k % 2) + w), pairs)
                last.then_inc(S["pe_up"], 1)

            def logits(c):
                pe.wait_ge(S["dve_A"], 7 + c)
                for i in range(4 * c, 4 * c + 4):
                    acc(PS[:, 4, i * NE:(i + 1) * NE], [(A[:, kt, i * P:(i + 1) * P], wgate[:, kt, :]) for kt in range(CT)], "pe_lg")

            pe.wait_ge(S["dve_x"], X_FFN + 2)
            logits(0)
            up(0)
            logits(1)
            up(1)
            pe.wait_ge(S["dve_ew"], 1)
            for i in range(NT):
                last = mm(PSB[:, 6 * HALF + i * P:6 * HALF + (i + 1) * P], ewt[:, i, 0:1].broadcast_to([P, P]), ident[:],
                          start=True, stop=True)
            last.then_inc(S["pe_ewb"], 1)
            pe.wait_ge(S["dve_ew"], 1)
            for i in range(NT):
                last = nc.tensor.transpose(PS[0:NE, 4 + i // 4, (i % 4) * P:(i % 4 + 1) * P], ewt[:, i, :], ident[:])
            last.then_inc(S["pe_ewt"], 1)
            for i in range(1, MT):
                up(2 * i)
                up(2 * i + 1)
                if i == 1:
                    pe.wait_ge(S["act_ewb"], 1)
                    pe.wait_ge(S["act_ewt"], 1)
                down(i - 1)
            down(MT - 1)


XBC_BANK = (2, 4, 6, 2, 4, 6)
MRING = 3
QRING = 3
FRAME = 5

X_ATT = NT
X_FFN = X_ATT + NT
X_SSD = X_FFN + 4


def arrange(x):
    import numpy as np
    f4 = np.float32

    def kt(w):
        return np.ascontiguousarray(w.reshape(-1, P, w.shape[-1]).transpose(1, 0, 2))

    def pv(v):
        return np.ascontiguousarray(v.reshape(-1, P).T)

    def rows(v):
        return np.ascontiguousarray(np.broadcast_to(v, (P,) + v.shape))

    o = {}
    o["xT"] = kt(x["x"].reshape(N, D).T)
    o["fT"] = kt(x["fside_BxSxS_0"].reshape(N, D).T).reshape(P, CT, NCH, HALF).transpose(0, 2, 1, 3).reshape(P, NCH, -1)
    o["condT"] = np.ascontiguousarray(x["cond_512"].T)
    mods = ("L0_cond", "L0_cond2", "L1_cond", "L1_cond2")
    o["wu"] = np.ascontiguousarray(np.stack([np.stack([pv(x[m + "_w"]), pv(x[m + "_u"])], 1) for m in mods], 1))
    att = [kt(x["L0_attn_" + n].T) for n in ("Wq", "Wk", "Wv", "Wo")]
    o["wqkvo"] = np.stack(att, 1)
    o["w1T"] = kt(x["L0_ffn_w1"].T).reshape(P, -1)
    o["w2T"] = kt(x["L0_ffn_w2"].T).reshape(P, -1)
    o["w3T"] = kt(x["L0_ffn_w3"].T).reshape(P, -1)
    o["gb"] = rows(np.concatenate([x["L0_ffn_g1"], x["L0_ffn_g2"], x["L0_ffn_g3"]]))
    w = x["L1_attn_in_proj_w"]
    jh = np.arange(SH).reshape(HG, 4).T.reshape(-1)
    o["inproj"] = kt(np.concatenate([w[:PROJ - SH], w[PROJ - SH:][jh]], 0).T)
    o["outproj"] = kt(x["L1_attn_out_proj_w"].T)
    o["convw"] = kt(x["L1_attn_conv_w"])
    o["convb"] = pv(x["L1_attn_conv_b"])
    o["dtb"] = rows(x["L1_attn_dt_bias"][jh])
    o["alog"] = rows(x["L1_attn_A_log"][jh])
    o["alogj"] = np.repeat(x["L1_attn_A_log"][jh].reshape(4, HG), Q, 0)
    o["dskip"] = pv(np.repeat(x["L1_attn_D"], SP_))
    o["normw"] = pv(x["L1_attn_norm_w"])
    o["wgate"] = kt(x["L1_ffn_w_gate"].T)

    def up(w):
        return w.reshape(MT, P, CT, P).transpose(0, 3, 2, 1).reshape(MT, P, D)
    dn = x["L1_ffn_w2"].transpose(0, 2, 1).reshape(MT, P, D)
    o["moe"] = np.concatenate([up(x["L1_ffn_w1"]), up(x["L1_ffn_w3"]), dn], 2)
    r = np.arange(P)
    o["ident"] = np.eye(P, dtype=f4)
    o["ones"] = np.ones((P, P), f4)
    o["negmask"] = np.where(r[None, :] > r[:, None], -3.3e38, 0.0).astype(f4)
    same = (r[:, None] // Q) == (r[None, :] // Q)
    o["ugt"] = (same & (r[:, None] > r[None, :])).astype(f4)
    o["tri"] = (same & (r[:, None] <= r[None, :])).astype(f4)
    o["cones"] = np.ascontiguousarray(np.broadcast_to(((r[:, None] // Q) == np.arange(NC)[None, :])[:, :, None], (P, NC, P))).astype(f4)
    o["step"] = ((r[:, None] % Q) <= np.arange(Q)[None, :]).astype(f4)
    o["notfirst"] = rows((np.arange(T) > 0).astype(f4))
    o["hmask"] = ((r[:, None] // HD) == np.arange(8)[None, :]).astype(f4)
    o["iota"] = rows(np.arange(NE, dtype=f4))
    return {k: np.ascontiguousarray(v) for k, v in o.items()}


def program(nc, arrays):
    args = {n: nc.dram_tensor("in_" + n, v.shape, mybir.dt.from_np(v.dtype), kind="ExternalInput").ap()
            for n, v in arrays.items()}
    out = nc.dram_tensor("out_0", (P, CT, N), mybir.dt.float32, kind="ExternalOutput").ap()
    routing = nc.dram_tensor("routing", (NE, N), mybir.dt.float32, kind="Internal").ap()
    build(nc, args, routing, out)


def kernel(**inputs):
    import numpy as np
    import concourse.bacc as bacc
    from concourse.bass_utils import run_bass_kernel_spmd

    arrays = arrange({k: np.asarray(v) for k, v in inputs.items()})
    nc = bacc.Bacc("TRN2", target_bir_lowering=False, num_devices=1)
    program(nc, arrays)
    r = run_bass_kernel_spmd(nc, [{"in_" + n: v for n, v in arrays.items()}], core_ids=[0])
    got = r.results[0]["out_0"]
    return np.ascontiguousarray(got.transpose(1, 0, 2).reshape(D, N).T).reshape(B, T, D)
```
